# Optimizing a Trainium2 kernel written in Bass

```python
import numpy as np
import jax
import jax.numpy as jnp

def _softmax(x, axis=-1):
    return jax.nn.softmax(x, axis=axis)

def _gelu(x):
    return jax.nn.gelu(x, approximate=True)

def _silu(x):
    return jax.nn.silu(x)

def _sigmoid(x):
    return jax.nn.sigmoid(x)

def _layernorm(x, axis=-1, eps=1e-05):
    m = jnp.mean(x, axis=axis, keepdims=True)
    v = jnp.var(x, axis=axis, keepdims=True)
    return (x - m) / jnp.sqrt(v + eps)

def _scatter_add(tgt, idx, src, axis=0):
    return tgt.at[idx].add(src)

def _segment_sum(src, seg, n):
    return jax.ops.segment_sum(src, seg, n)
kernel_name = 'mk_conv_seq_d4_conv_nchw256_r2_d788b9'

def setup_inputs(seed: int=0):
    np.random.seed(seed)
    _w = jnp.asarray

    def _rec_inputs():
        import jax
        import jax.numpy as jnp
        _gk = jax.random.key(seed)
        x = -0.0005207 + 1.001 * jax.random.normal(jax.random.fold_in(_gk, 1), (2, 128, 32, 32), jnp.float32)
        return x
    x = _rec_inputs()

    def _L0_conv_setup():
        import jax, jax.numpy as jnp
        import numpy as np
        IN_DIM = 128
        AT_DIM = 128
        NUM_HEAD = 4
        COMPRESS_QK = 8
        D_QK = AT_DIM // NUM_HEAD // COMPRESS_QK
        AT_HEAD = AT_DIM // NUM_HEAD
        B, H, W = (2, 32, 32)
        key = jax.random.key(seed)
        ks = jax.random.split(key, 11)
        s = 0.02
        x = jax.random.normal(ks[0], (B, IN_DIM, H, W), dtype=jnp.float32)
        Wq = jax.random.normal(ks[1], (NUM_HEAD, D_QK, IN_DIM), dtype=jnp.float32) * s
        bq = jax.random.normal(ks[2], (NUM_HEAD, D_QK), dtype=jnp.float32) * s
        Wk = jax.random.normal(ks[3], (NUM_HEAD, D_QK, IN_DIM), dtype=jnp.float32) * s
        bk = jax.random.normal(ks[4], (NUM_HEAD, D_QK), dtype=jnp.float32) * s
        Wv = jax.random.normal(ks[5], (NUM_HEAD, D_QK, IN_DIM), dtype=jnp.float32) * s
        bv = jax.random.normal(ks[6], (NUM_HEAD, D_QK), dtype=jnp.float32) * s
        Wo = jax.random.normal(ks[7], (NUM_HEAD, AT_HEAD, D_QK), dtype=jnp.float32) * s
        bo = jax.random.normal(ks[8], (NUM_HEAD, AT_HEAD), dtype=jnp.float32) * s
        gamma = jax.random.normal(ks[9], (NUM_HEAD,), dtype=jnp.float32)
        return {'x': x, 'Wq': Wq, 'bq': bq, 'Wk': Wk, 'bk': bk, 'Wv': Wv, 'bv': bv, 'Wo': Wo, 'bo': bo, 'gamma': gamma}
    _L0_conv_all = _L0_conv_setup()
    _L0_conv_in = {k: v for k, v in _L0_conv_all.items() if k in ('Wq', 'bq', 'Wk', 'bk', 'Wv', 'bv', 'Wo', 'bo', 'gamma')}
    del _L0_conv_all

    def _L1_conv_setup():
        import jax, jax.numpy as jnp
        import numpy as np
        C = 128
        C8 = C // 8
        B, H, W = (8, 32, 32)
        key = jax.random.key(seed)
        ks = jax.random.split(key, 8)
        scale = 1.0 / np.sqrt(C)
        return {'x': jax.random.normal(ks[0], (B, C, H, W), dtype=jnp.float32), 'wq': jax.random.normal(ks[1], (C8, C), dtype=jnp.float32) * scale, 'bq': jax.random.normal(ks[2], (C8,), dtype=jnp.float32) * 0.01, 'wk': jax.random.normal(ks[3], (C8, C), dtype=jnp.float32) * scale, 'bk': jax.random.normal(ks[4], (C8,), dtype=jnp.float32) * 0.01, 'wv': jax.random.normal(ks[5], (C, C), dtype=jnp.float32) * scale, 'bv': jax.random.normal(ks[6], (C,), dtype=jnp.float32) * 0.01, 'gamma': jax.random.normal(ks[7], (1,), dtype=jnp.float32) * 0.1}
    _L1_conv_all = _L1_conv_setup()
    _L1_conv_in = {k: v for k, v in _L1_conv_all.items() if k in ('wq', 'bq', 'wk', 'bk', 'wv', 'bv', 'gamma')}
    del _L1_conv_all

    def _L2_conv_setup():
        import jax, jax.numpy as jnp
        import numpy as np
        C = 128
        H_HEADS = 8
        R = 2
        EPS = 1e-05
        G = 8

        def group_norm(x, w, b):
            B, C_, H, W = x.shape
            xg = x.reshape(B, G, C_ // G, H, W)
            mu = xg.mean(axis=(2, 3, 4), keepdims=True)
            var = xg.var(axis=(2, 3, 4), keepdims=True)
            xn = ((xg - mu) * jax.lax.rsqrt(var + EPS)).reshape(B, C_, H, W)
            return xn * w[None, :, None, None] + b[None, :, None, None]

        def conv1x1(x, w):
            return jnp.einsum('oc,bchw->bohw', w, x)

        def avg_pool2(x):
            B, C_, H, W = x.shape
            return x.reshape(B, C_, H // R, R, W // R, R).mean(axis=(3, 5))
        key = jax.random.key(seed)
        ks = jax.random.split(key, 9)
        s = 0.05
        return {'x': jax.random.normal(ks[0], (4, C, 32, 32), dtype=jnp.float32), 'wq': jax.random.normal(ks[1], (C, C), dtype=jnp.float32) * s, 'wk': jax.random.normal(ks[2], (C, C), dtype=jnp.float32) * s, 'wv': jax.random.normal(ks[3], (C, C), dtype=jnp.float32) * s, 'wproj': jax.random.normal(ks[4], (C, C), dtype=jnp.float32) * s, 'gnq_w': jnp.ones((C,), jnp.float32), 'gnq_b': jnp.zeros((C,), jnp.float32), 'gnk_w': jnp.ones((C,), jnp.float32), 'gnk_b': jnp.zeros((C,), jnp.float32)}
    _L2_conv_all = _L2_conv_setup()
    _L2_conv_in = {k: v for k, v in _L2_conv_all.items() if k in ('wq', 'wk', 'wv', 'wproj', 'gnq_w', 'gnq_b', 'gnk_w', 'gnk_b')}
    del _L2_conv_all

    def _L3_conv_setup():
        import jax, jax.numpy as jnp
        import numpy as np
        GROUPS = 32
        EPS = 1e-05
        key = jax.random.key(seed)
        ks = jax.random.split(key, 3)
        b, c, h, w = (4, 128, 32, 32)
        x = jax.random.normal(ks[0], (b, c, h, w), dtype=jnp.float32)
        gn_w = jnp.ones((c,), jnp.float32)
        gn_b = jnp.zeros((c,), jnp.float32)
        qkv_w = jax.random.normal(ks[1], (3 * c, c), jnp.float32) * (1.0 / np.sqrt(c))
        qkv_b = jnp.zeros((3 * c,), jnp.float32)
        out_w = jax.random.normal(ks[2], (c, c), jnp.float32) * (1.0 / np.sqrt(c))
        out_b = jnp.zeros((c,), jnp.float32)
        return {'x': x, 'gn_w': gn_w, 'gn_b': gn_b, 'qkv_w': qkv_w, 'qkv_b': qkv_b, 'out_w': out_w, 'out_b': out_b}
    _L3_conv_all = _L3_conv_setup()
    _L3_conv_in = {k: v for k, v in _L3_conv_all.items() if k in ('gn_w', 'gn_b', 'qkv_w', 'qkv_b', 'out_w', 'out_b')}
    del _L3_conv_all
    return {'x': x, 'L0_conv_Wq': _L0_conv_in['Wq'], 'L0_conv_bq': _L0_conv_in['bq'], 'L0_conv_Wk': _L0_conv_in['Wk'], 'L0_conv_bk': _L0_conv_in['bk'], 'L0_conv_Wv': _L0_conv_in['Wv'], 'L0_conv_bv': _L0_conv_in['bv'], 'L0_conv_Wo': _L0_conv_in['Wo'], 'L0_conv_bo': _L0_conv_in['bo'], 'L0_conv_gamma': _L0_conv_in['gamma'], 'L1_conv_wq': _L1_conv_in['wq'], 'L1_conv_bq': _L1_conv_in['bq'], 'L1_conv_wk': _L1_conv_in['wk'], 'L1_conv_bk': _L1_conv_in['bk'], 'L1_conv_wv': _L1_conv_in['wv'], 'L1_conv_bv': _L1_conv_in['bv'], 'L1_conv_gamma': _L1_conv_in['gamma'], 'L2_conv_wq': _L2_conv_in['wq'], 'L2_conv_wk': _L2_conv_in['wk'], 'L2_conv_wv': _L2_conv_in['wv'], 'L2_conv_wproj': _L2_conv_in['wproj'], 'L2_conv_gnq_w': _L2_conv_in['gnq_w'], 'L2_conv_gnq_b': _L2_conv_in['gnq_b'], 'L2_conv_gnk_w': _L2_conv_in['gnk_w'], 'L2_conv_gnk_b': _L2_conv_in['gnk_b'], 'L3_conv_gn_w': _L3_conv_in['gn_w'], 'L3_conv_gn_b': _L3_conv_in['gn_b'], 'L3_conv_qkv_w': _L3_conv_in['qkv_w'], 'L3_conv_qkv_b': _L3_conv_in['qkv_b'], 'L3_conv_out_w': _L3_conv_in['out_w'], 'L3_conv_out_b': _L3_conv_in['out_b']}

def reference(x, L0_conv_Wq, L0_conv_bq, L0_conv_Wk, L0_conv_bk, L0_conv_Wv, L0_conv_bv, L0_conv_Wo, L0_conv_bo, L0_conv_gamma, L1_conv_wq, L1_conv_bq, L1_conv_wk, L1_conv_bk, L1_conv_wv, L1_conv_bv, L1_conv_gamma, L2_conv_wq, L2_conv_wk, L2_conv_wv, L2_conv_wproj, L2_conv_gnq_w, L2_conv_gnq_b, L2_conv_gnk_w, L2_conv_gnk_b, L3_conv_gn_w, L3_conv_gn_b, L3_conv_qkv_w, L3_conv_qkv_b, L3_conv_out_w, L3_conv_out_b):
    import jax
    import jax.numpy as jnp

    def _L0_conv_ref(x, Wq, bq, Wk, bk, Wv, bv, Wo, bo, gamma):
        import jax, jax.numpy as jnp
        import numpy as np
        IN_DIM = 128
        AT_DIM = 128
        NUM_HEAD = 4
        COMPRESS_QK = 8
        D_QK = AT_DIM // NUM_HEAD // COMPRESS_QK
        AT_HEAD = AT_DIM // NUM_HEAD
        B, H, W = (2, 32, 32)
        b, C, h, w = x.shape
        N = h * w
        xf = x.reshape(b, C, N)
        q = jnp.einsum('hdc,bcn->bhdn', Wq, xf) + bq[None, :, :, None]
        k = jnp.einsum('hdc,bcn->bhdn', Wk, xf) + bk[None, :, :, None]
        v = jnp.einsum('hdc,bcn->bhdn', Wv, xf) + bv[None, :, :, None]
        S = jnp.einsum('bhdn,bhdm->bhnm', q, k)
        A = jax.nn.softmax(S, axis=-2)
        o = jnp.einsum('bhdn,bhnm->bhdm', v, A)
        y = jnp.einsum('hed,bhdm->bhem', Wo, o) + bo[None, :, :, None]
        y = gamma[None, :, None, None] * y
        out = y.reshape(b, NUM_HEAD * AT_HEAD, h, w) + x
        return out

    def _L1_conv_ref(x, wq, bq, wk, bk, wv, bv, gamma):
        import jax, jax.numpy as jnp
        import numpy as np
        C = 128
        C8 = C // 8
        B, H, W = (8, 32, 32)
        b, c, h, w = x.shape
        n = h * w
        xf = x.reshape(b, c, n)
        q = jnp.einsum('oc,bcn->bno', wq, xf) + bq
        k = jnp.einsum('oc,bcn->bon', wk, xf) + bk[:, None]
        v = jnp.einsum('oc,bcn->bon', wv, xf) + bv[:, None]
        attn = jax.nn.softmax(jnp.einsum('bno,bom->bnm', q, k), axis=2)
        out = jnp.einsum('bcm,bnm->bcn', v, attn).reshape(b, c, h, w)
        return x + gamma[0] * out

    def _L2_conv_ref(x, wq, wk, wv, wproj, gnq_w, gnq_b, gnk_w, gnk_b):
        import jax, jax.numpy as jnp
        import numpy as np
        C = 128
        H_HEADS = 8
        R = 2
        EPS = 1e-05
        G = 8

        def group_norm(x, w, b):
            B, C_, H, W = x.shape
            xg = x.reshape(B, G, C_ // G, H, W)
            mu = xg.mean(axis=(2, 3, 4), keepdims=True)
            var = xg.var(axis=(2, 3, 4), keepdims=True)
            xn = ((xg - mu) * jax.lax.rsqrt(var + EPS)).reshape(B, C_, H, W)
            return xn * w[None, :, None, None] + b[None, :, None, None]

        def conv1x1(x, w):
            return jnp.einsum('oc,bchw->bohw', w, x)

        def avg_pool2(x):
            B, C_, H, W = x.shape
            return x.reshape(B, C_, H // R, R, W // R, R).mean(axis=(3, 5))
        B, C_, H, W = x.shape
        h = H_HEADS
        d = C_ // h
        scale = d ** (-0.5)
        q = conv1x1(group_norm(x, gnq_w, gnq_b), wq).reshape(B, h, d, H * W)
        kv = avg_pool2(x)
        hk, wk_ = kv.shape[-2:]
        kvn = group_norm(kv, gnk_w, gnk_b)
        k = conv1x1(kvn, wk).reshape(B, h, d, hk * wk_)
        v = conv1x1(kvn, wv).reshape(B, h, d, hk * wk_)
        attn = jnp.einsum('bhdq,bhdk->bhqk', q, k) * scale
        attn = jax.nn.softmax(attn, axis=-1)
        y = jnp.einsum('bhqk,bhdk->bhdq', attn, v).reshape(B, C_, H, W)
        return x + conv1x1(y, wproj)

    def _L3_conv_ref(x, gn_w, gn_b, qkv_w, qkv_b, out_w, out_b):
        import jax, jax.numpy as jnp
        import numpy as np
        GROUPS = 32
        EPS = 1e-05
        b, c, h, w = x.shape
        scale = c ** (-0.5)
        xg = x.reshape(b, GROUPS, c // GROUPS, h, w)
        mean = xg.mean(axis=(2, 3, 4), keepdims=True)
        var = xg.var(axis=(2, 3, 4), keepdims=True)
        xn = ((xg - mean) * jax.lax.rsqrt(var + EPS)).reshape(b, c, h, w)
        xn = xn * gn_w[None, :, None, None] + gn_b[None, :, None, None]
        qkv = jnp.einsum('bchw,oc->bohw', xn, qkv_w) + qkv_b[None, :, None, None]
        q, k, v = jnp.split(qkv, 3, axis=1)
        to_seq = lambda t: t.reshape(b, c, h * w).transpose(0, 2, 1)
        q, k, v = (to_seq(q), to_seq(k), to_seq(v))
        sim = jnp.einsum('bic,bjc->bij', q, k) * scale
        attn = jax.nn.softmax(sim, axis=-1)
        out = jnp.einsum('bij,bjc->bic', attn, v)
        out = out.transpose(0, 2, 1).reshape(b, c, h, w)
        out = jnp.einsum('bchw,oc->bohw', out, out_w) + out_b[None, :, None, None]
        return out + x

    def _gn(v, G=32, eps=1e-05):
        B_, C_, H_, W_ = v.shape
        g = v.reshape(B_, G, C_ // G, H_, W_)
        m = jnp.mean(g, axis=(2, 3, 4), keepdims=True)
        s = jnp.var(g, axis=(2, 3, 4), keepdims=True)
        return ((g - m) / jnp.sqrt(s + eps)).reshape(v.shape)

    def _ln_c(v, eps=1e-06):
        m = jnp.mean(v, axis=1, keepdims=True)
        s = jnp.var(v, axis=1, keepdims=True)
        return (v - m) / jnp.sqrt(s + eps)

    def _ln_t(v, eps=1e-05):
        m = jnp.mean(v, axis=-1, keepdims=True)
        s = jnp.var(v, axis=-1, keepdims=True)
        return (v - m) / jnp.sqrt(s + eps)

    def _to_tokens(v):
        B_, C_, H_, W_ = v.shape
        return v.reshape(B_, C_, H_ * W_).transpose(0, 2, 1)

    def _from_tokens(t, like):
        B_, C_, H_, W_ = like.shape
        return t.transpose(0, 2, 1).reshape(B_, C_, H_, W_)
    x = _L0_conv_ref(x, L0_conv_Wq, L0_conv_bq, L0_conv_Wk, L0_conv_bk, L0_conv_Wv, L0_conv_bv, L0_conv_Wo, L0_conv_bo, L0_conv_gamma)
    x = _L1_conv_ref(x, L1_conv_wq, L1_conv_bq, L1_conv_wk, L1_conv_bk, L1_conv_wv, L1_conv_bv, L1_conv_gamma)
    x = _L2_conv_ref(x, L2_conv_wq, L2_conv_wk, L2_conv_wv, L2_conv_wproj, L2_conv_gnq_w, L2_conv_gnq_b, L2_conv_gnk_w, L2_conv_gnk_b)
    x = _L3_conv_ref(x, L3_conv_gn_w, L3_conv_gn_b, L3_conv_qkv_w, L3_conv_qkv_b, L3_conv_out_w, L3_conv_out_b)
    return x

_drawn_inputs = setup_inputs


def setup_inputs(seed=0):
    import zlib

    import numpy as np

    out = dict(_drawn_inputs(seed))
    spreads = {'L2_conv_gnq_w': (1.0, 0.6),
     'L2_conv_gnq_b': (0.0, 0.8),
     'L2_conv_gnk_w': (1.0, 0.6),
     'L2_conv_gnk_b': (0.0, 0.342),
     'L3_conv_gn_w': (1.0, 0.2),
     'L3_conv_gn_b': (0.0, 0.1),
     'L3_conv_qkv_b': (0.0, 0.1),
     'L3_conv_out_b': (0.0, 0.1)}
    factors = {'L0_conv_Wq': 8.0,
     'L0_conv_bq': 64.0,
     'L0_conv_Wk': 8.0,
     'L0_conv_bk': 8.0,
     'L0_conv_Wv': 8.0,
     'L0_conv_bv': 8.0,
     'L0_conv_Wo': 8.0,
     'L0_conv_bo': 3.521,
     'L0_conv_gamma': 3.843,
     'L1_conv_wq': 8.0,
     'L1_conv_bq': 52.427,
     'L1_conv_wk': 8.0,
     'L1_conv_bk': 64.0,
     'L1_conv_wv': 8.0,
     'L1_conv_bv': 64.0,
     'L2_conv_wq': 4.103,
     'L2_conv_wk': 4.076}
    for name, (base, spread) in spreads.items():
        noise = np.random.default_rng([zlib.crc32(name.encode()), seed]).standard_normal(out[name].shape)
        drawn = base * np.exp(spread * noise) if base else spread * noise
        out[name] = jnp.asarray(drawn.astype(out[name].dtype))
    for name, factor in factors.items():
        out[name] = (out[name] * factor).astype(out[name].dtype)
    return out
```

```python
from contextlib import ExitStack

import concourse.bass as bass
from concourse import mybir

F32 = mybir.dt.float32
F32R = mybir.dt.float32r
I32 = mybir.dt.int32
ALU = mybir.AluOpType
ACT = mybir.ActivationFunctionType
AX = mybir.AxisListType

B, C, N = 2, 128, 1024
NT = N // 128
HALF = 512
NKV = 256
H0, D0 = 4, 4
D1 = 16
H2, D2 = 8, 16
HG = 4
MAXROW = 64
KROWS = 96
RING = 3
NP = 8
EPS = 1e-5
SCALE = {0: 1.0, 1: 1.0, 2: float(D2) ** -0.5, 3: float(C) ** -0.5}
RSQRT_SEED = 0x5F3759DF

FIRST = [("w0qk", 32), ("b0qk", 1), ("w0v", 16), ("b0v", 16), ("x0den", 1), ("gam0", 4), ("gam0c", 1),
         ("b0o", 1), ("w0o", 128), ("ident", 128)]
REST = [("sel", 1024), ("w1qk", 32), ("b1qk", 1), ("w1v", 128), ("b1v", 1), ("gam1", 1),
        ("w2q", 128), ("w2k", 128), ("w2v", 128), ("w2p", 256), ("gn2", 4), ("avg16", 128),
        ("sel2", 4), ("ones4", 4), ("w3q", 128), ("w3k", 128), ("w3v", 128), ("w3o", 128), ("b3q", 1),
        ("b3k", 1), ("b3v", 1), ("b3o", 1), ("gn3", 2), ("avg4", 128)]


def columns(layout):
    at, out = 0, {}
    for name, width in layout:
        out[name] = (at, width)
        at += width
    return out, at


UNITS = [(0, 0, 0), (0, 0, 1), (0, 0, 2), (0, 0, 3), (0, 1, 0), (0, 1, 1), (1, 0, 0), (0, 1, 2),
         (0, 1, 3), (2, 0, 0), (2, 0, 1), (1, 1, 0), (3, 0, 0), (2, 1, 0), (2, 1, 1), (3, 1, 0)]
GROUPS = {0: 4, 1: 1, 2: 2, 3: 1}
LEAD = 12


def prologue(L, b):
    if L == 0:
        return [("qk", L, b), ("v", L, b)]
    if L == 1:
        return [("qk", L, b), ("v", L, b)]
    if L == 2:
        return [("stats", L, b), ("norm", L, b), ("q", L, b), ("k", L, b), ("v", L, b)]
    return [("stats", L, b), ("norm", L, b), ("q", L, b), ("k", L, b), ("v", L, b)]


def epilogue(L, b, g):
    if L == 0:
        return [("den", L, b, g), ("y", L, b), ("rows", L, b, g), ("bcast", L, b, g)] if g == 3 else []
    if L == 2:
        return [("den", L, b, g), ("rows", L, b, g), ("bcast", L, b, g)] + ([("y", L, b)] if g == 1 else [])
    return [("den", L, b, g), ("rows", L, b, g), ("bcast", L, b, g)]


def last_step(L, b):
    return ("y", L, b) if L == 2 else ("bcast", L, b, GROUPS[L] - 1)


def build_plan():
    ahead = []
    for u, (L, b, g) in enumerate(UNITS):
        if g == 0:
            ahead += [(u, 0, s) for s in prologue(L, b)]
        ahead += [(u, t, ("A", L, b, g, t)) for t in range(8)] + [(u, 8, ("split", L, b, g))]
    plan, pv, ends, at = [("fold", 3)], [], [], 0

    def allowed():
        s = ahead[at][2]
        return s[0] not in ("qk", "stats") or s[1] == 0 or last_step(s[1] - 1, s[2]) in plan

    def tail_step():
        if pv:
            s = pv.pop(0)[1]
            plan.append(s)
            if s[0] == "out":
                ends.extend(epilogue(*s[1:]))
        else:
            plan.append(ends.pop(0))

    for k, (L, b, g) in enumerate(UNITS):
        while at < len(ahead) and ahead[at][0] <= k:
            while not allowed():
                tail_step()
            plan.append(ahead[at][2])
            at += 1
        if ("top", L, b, g) not in plan:
            plan.append(("top", L, b, g))
        for t in range(8):
            plan.append(("B", L, b, g, t))
            n = 8 * k + t
            if L in (0, 2):
                if t % 4 == 3:
                    pv.append((n + 2, ("PV4", L, b, g, t // 4)))
            else:
                pv.append((n + 2, ("PV1", L, b, g, t)))
            if t == 7:
                pv.append((n + 2, ("out", L, b, g)))
            burst = 0
            while at < len(ahead) and burst < 2 and allowed() and 8 * ahead[at][0] + ahead[at][1] <= n + LEAD:
                plan.append(ahead[at][2])
                burst += 1
                at += 1
            for v in UNITS[k + 1:k + 3]:
                if ("split",) + v in plan[:-2] and ("top",) + v not in plan:
                    plan.append(("top",) + v)
            if ends:
                plan.append(ends.pop(0))
            while pv and pv[0][0] <= n:
                tail_step()
    while pv or ends:
        tail_step()
    return plan


def attention_layers(nc, x, first, rest, out):
    plan = build_plan()
    assert len(set(plan)) == len(plan)

    def last_reader(s):
        kind, L = s[0], s[1]
        if kind in ("A", "norm", "den", "bcast", "qk", "q", "k") or (kind, L) in (("v", 0), ("y", 2)):
            return "dve"
        if kind in ("B", "top", "rows", "fold") or (kind, L) in (("v", 1), ("v", 2), ("v", 3), ("y", 0)):
            return "act"
        return None

    jobs = [s for s in plan if last_reader(s)]
    job = {s: n for n, s in enumerate(jobs)}
    read = {}
    for who in ("dve", "act"):
        for n, s in enumerate([s for s in jobs if last_reader(s) == who]):
            read[s] = n + 1

    def number(kinds, layers=(0, 1, 2, 3)):
        return {s: n for n, s in enumerate([s for s in plan if s[0] in kinds and s[1] in layers])}

    b_no = number(("B",))
    b_order = list(b_no)
    hi_no = number(("qk", "q", "k"))
    stage = [s for s in plan if s[0] in ("qk", "q") and s[1] < 3]
    top_no = number(("top",))
    split_no = number(("split",))
    out_no = number(("out",))
    x_no = {}
    for s in plan:
        if s[0] == "bcast" and s[1] != 2 and s == last_step(s[1], s[2]):
            x_no[(s[1], s[2])] = len(x_no) + 1
    den_ops = [s for s in plan if s[0] == "B" and s[1] in (1, 3) and s[4] > 0]
    den_no = {s: n + 1 for n, s in enumerate(den_ops)}
    o_tile = {u: (u[2] if u[0] == 0 else {(1, 0): 4, (1, 1): 2, (3, 0): 3, (3, 1): 2}.get(u[:2], u[2]))
              for u in UNITS}
    pv_done_at = {}
    n = 0
    for s in plan:
        if s[0] == "PV4":
            for t in range(4 * s[4], 4 * s[4] + 4):
                n += 1
                pv_done_at[("B", *s[1:4], t)] = n
        elif s[0] == "PV1":
            n += 1
            pv_done_at[("B", *s[1:4], s[4])] = n

    col1, n1 = columns(FIRST)
    col2, n2 = columns(REST)

    with ExitStack() as ctx:
        def sb(name, shape, dt=F32):
            return ctx.enter_context(nc.sbuf_tensor(name, shape, dt))

        def sem(name):
            return ctx.enter_context(nc.semaphore(name))

        w1 = sb("w1", [128, n1])
        w2 = sb("w2", [128, n2])

        def w(name):
            a, width = (col1 if name in col1 else col2)[name]
            return (w1 if name in col1 else w2)[:, a:a + width]

        X = [sb(f"x{b}", [C, N]) for b in range(B)]
        ST = [sb(f"score_ops{b}", [128, 10, N], F32R) for b in range(B)]
        Hs = sb("stage_hi", [128, N], F32R)
        Ls = sb("stage_lo", [128, N], F32R)
        HK = sb("stage_k_hi", [128, NKV], F32R)
        LK = sb("stage_k_lo", [128, NKV], F32R)
        P = sb("probs", [128, NP, N])
        V0 = [sb(f"v0_{b}", [128, H0, NT, 32]) for b in range(B)]
        V2 = [sb(f"v2_{b}", [128, 2, 2, HG, 32]) for b in range(B)]
        V13 = [sb(f"v13_{b}", [128, NT, C]) for b in range(B)]
        O = [sb(f"attn_out{i}", [128, N]) for i in range(5)]
        DS = sb("prob_sum", [128, N])
        T = sb("tmp", [128, N])
        XN = sb("x_norm", [C, N])
        KV = sb("kv_pool", [C, NKV])
        KP = XN[:, 0:512]
        KVN = sb("kv_norm", [C, NKV])
        NM = sb("neg_max", [128, 2, 32])
        ZT = sb("max_halves", [128, 2, 2, 32])
        ZR = sb("max_rows", [64, 2, 128])
        RC = sb("recip_cols", [128, 128])
        RT = sb("recip_rows", [128, 128])
        const = sb("const_rows", [2, 2, N])
        pick = sb("max_picker", [KROWS, 128], F32R)
        w3vo = sb("w3vo", [C, C])
        b3eff = sb("b3eff", [C, 1])
        gb0 = sb("gamma_bo", [C, 1])
        gb1 = sb("gamma_bv", [C, 1])
        bn = sb("bn_parts", [C, 3, 6])
        mv = sb("mean_var", [C, 2, 2])
        gs = sb("group_stats", [C, 2, 2])
        nt = sb("norm_tmp", [C, 6, 2])
        ab = sb("norm_scale_shift", [C, 2, 2])

        ps = ctx.enter_context(nc.psum_tensor("products", [128, RING, N], F32))
        acc = ctx.enter_context(nc.psum_tensor("attn_acc", [128, N], F32))

        x_in = [sem(f"x_in{b}") for b in range(B)]
        w1_in, w2_in = sem("w1_in"), sem("w2_in")
        cleared_dve, cleared_pool = sem("cleared_dve"), sem("cleared_pool")
        consts_ready = sem("consts_ready")
        tile_full = sem("tile_full")
        read_dve, read_act = sem("tile_read_dve"), sem("tile_read_act")
        hi_done = sem("hi_done")
        stacks_in = [sem(f"stacks_in{b}") for b in range(B)]
        split_done = sem("split_done")
        maxrows_in = [sem(f"maxrows_in{b}") for b in range(B)]
        pv_done = sem("pv_done")
        den_acc = sem("den_acc")
        acc_out = sem("acc_out")
        x_upd = sem("x_upd")
        stats_done = sem("stats_done")
        pooled = sem("pooled")
        coef_done = sem("coef_done")
        xn_done, kvn_done = sem("xn_done"), sem("kvn_done")
        dve_chain = sem("dve_chain")
        pool_chain = sem("pool_chain")
        out_done = sem("out_done")

        def slot(s):
            return ps[:, job[s] % RING, :]

        def wait_tile(eng, s):
            eng.wait_ge(tile_full, job[s] + 1)

        def wait_read(eng, s):
            eng.wait_ge(read_dve if last_reader(s) == "dve" else read_act, read[s])

        def wait_x(eng, L, b):
            if L == 0:
                eng.wait_ge(x_in[b], 16)
            elif L == 3:
                wait_read(eng, ("y", 2, b))
            else:
                eng.wait_ge(x_upd, x_no[(L - 1, b)])

        stack_dmas = {0: 9, 1: 9, 2: 9}

        def stacks_count(L, b):
            return 16 * sum(stack_dmas[i] for i in range(min(L, 2) + 1))

        def wait_stage_free(eng, s):
            i = stage.index(s)
            if i:
                p = stage[i - 1]
                eng.wait_ge(stacks_in[p[2]], stacks_count(p[1], p[2]))

        def wait_ops_free(eng, L, b):
            if L == 0:
                eng.wait_ge(cleared_pool, 6 if b == 0 else 8)
                eng.wait_ge(cleared_dve, 2)
            else:
                wait_tile(eng, ("B", L - 1, b, GROUPS[L - 1] - 1, 7))

        def max_count(L, b, g):
            order = [s for s in top_no if s[2] == b]
            return 16 * (order.index(("top", L, b, g)) + 1)

        def previous(kind, s):
            found = [p for p in plan[:plan.index(s)] if p[0] == kind]
            return found[-1] if found else None

        def x_upd_before(s):
            return len([p for p in plan[:plan.index(s)] if p[0] == "bcast" and p[1] != 2])

        norm_no = number(("norm",))

        block = ctx.enter_context(nc.Block())

        @block.sync
        def _(sp):
            sp.dma_start(w1[:, :], first).then_inc(w1_in, 16)
            sp.dma_start(X[0][:, :], x[0]).then_inc(x_in[0], 16)
            sp.dma_start(X[1][:, :], x[1]).then_inc(x_in[1], 16)
            sp.dma_start(w2[:, :], rest).then_inc(w2_in, 16)

            def spread(b, rows, r0, slots, parts, kept):
                hi, lo = parts
                d = rows
                for r, src in enumerate((hi, lo, hi, lo) if kept else (hi, hi, lo, lo)):
                    dst = slots(d * r, d * r + d)
                    sp.dma_start(dst, src).then_inc(stacks_in[b], 16)

            for s in plan:
                kind, L, b = s[0], s[1], s[2] if len(s) > 2 else None
                if kind == "qk" or (kind in ("q", "k") and L == 2):
                    sp.wait_ge(hi_done, hi_no[s] + 1)
                    wait_read(sp, s)
                    wait_ops_free(sp, L, b)
                S = ST[b][:, :, :].bitcast(F32) if b is not None else None
                if kind == "qk":
                    d, heads = (D0, H0) if L == 0 else (D1, 1)
                    for kept in (True, False):
                        r0 = 0 if kept else 16
                        s0 = 0 if kept else 4
                        spread(b, d, r0, lambda a, z: S[a:z, s0:s0 + heads, :],
                               (Hs[r0:r0 + 16, :].bitcast(F32), Ls[r0:r0 + 16, :].bitcast(F32)), kept)
                    if L == 0:
                        sp.dma_start(S[MAXROW:MAXROW + 2, 4:8, :],
                                     const[:, 1:2, :].broadcast_to([2, 4, N])).then_inc(stacks_in[b], 16)
                    else:
                        sp.dma_start(S[MAXROW:MAXROW + 2, 0:1, :], const[:, 0:1, :]).then_inc(stacks_in[b], 16)
                elif kind == "q" and L == 2:
                    spread(b, D2, 0, lambda a, z: S[a:z, 0:H2, :], (Hs[:, :].bitcast(F32), Ls[:, :].bitcast(F32)), True)
                    sp.dma_start(S[MAXROW:MAXROW + 2, 0:H2, :],
                                 const[:, 0:1, :].broadcast_to([2, H2, N])).then_inc(stacks_in[b], 16)
                elif kind == "k" and L == 2:
                    spread(b, D2, 0,
                           lambda a, z: S[a:z, 8:10, :].rearrange("p s n -> p (s n)").rearrange("p (h n) -> p h n", h=H2),
                           (HK[:, :].bitcast(F32), LK[:, :].bitcast(F32)), False)
                elif kind == "top":
                    g = s[3]
                    i = top_no[s] % 2
                    wait_read(sp, s)
                    k0, kn = {0: (g, 1), 1: (0, 1), 2: (HG * g, HG), 3: (2, 1)}[L]
                    sp.dma_start(S[MAXROW:MAXROW + 2, k0:k0 + kn, :], ZR[0:16 * kn, i, :]).then_inc(maxrows_in[b], 16)
                elif kind == "bcast" and L == 3:
                    sp.wait_ge(x_upd, x_no[(3, b)])
                    sp.dma_start(out[b], X[b][:, :]).then_inc(out_done, 16)
            sp.wait_ge(out_done, 16 * B)

        @block.gpsimd
        def _(pool):
            nc.gpsimd.memset(ST[0][:, 2:4, :].bitcast(F32), 0.0).then_inc(cleared_pool, 1)
            nc.gpsimd.memset(ST[0][:, 6:8, :].bitcast(F32), 0.0).then_inc(cleared_pool, 1)
            nc.gpsimd.memset(const[:, 0, :], 0.0).then_inc(cleared_pool, 1)
            nc.gpsimd.memset(const[:, 1, :], 1.0).then_inc(cleared_pool, 1)
            nc.gpsimd.memset(V0[0][:, :, :, :], 0.0).then_inc(cleared_pool, 1)
            pool.wait_ge(cleared_pool, 5)
            nc.gpsimd.memset(V0[0][:, :, :, D0:D0 + 1], 1.0).then_inc(cleared_pool, 1)
            nc.gpsimd.memset(ST[1][:, 0:8, :].bitcast(F32), 0.0).then_inc(cleared_pool, 1)
            nc.gpsimd.memset(V0[1][:, :, :, :], 0.0).then_inc(cleared_pool, 1)
            for b in range(B):
                nc.gpsimd.memset(ST[b][:, 8:10, :].bitcast(F32), 0.0).then_inc(cleared_pool, 1)
                nc.gpsimd.memset(V2[b][:, :, :, :, :], 0.0).then_inc(cleared_pool, 1)
            nc.gpsimd.memset(pick[:, :].bitcast(F32), 0.0).then_inc(cleared_pool, 1)
            nc.gpsimd.memset(RC[:, :], 0.0).then_inc(cleared_pool, 1)
            pool.wait_ge(cleared_pool, 14)
            nc.gpsimd.memset(V0[1][:, :, :, D0:D0 + 1], 1.0).then_inc(cleared_pool, 1)
            for b in range(B):
                nc.gpsimd.memset(V2[b][:, :, :, :, D2:D2 + 1], 1.0).then_inc(cleared_pool, 1)
            ones = [ST[b][MAXROW:MAXROW + 2, 8:10, :].bitcast(F32) for b in range(B)] + [
                pick[MAXROW:MAXROW + 2, :].bitcast(F32)]
            for i, m in enumerate(ones):
                pool.wait_ge(cleared_pool, 17 + i)
                nc.gpsimd.memset(m, 1.0).then_inc(cleared_pool, 1)
            pool.wait_ge(cleared_pool, 20)
            links = 0
            prev_den = None
            for s in plan:
                kind, L, b = s[0], s[1], s[2] if len(s) > 2 else None
                if s in den_no:
                    t = s[4]
                    n = b_no[s]
                    wait_read(pool, s)
                    if t == 1:
                        if prev_den:
                            wait_tile(pool, prev_den)
                        prev_den = ("den", L, b, 0)
                        first_in = P[:, (n - 1) % NP, :]
                    else:
                        pool.wait_ge(den_acc, den_no[s] - 1)
                        first_in = DS[:, :]
                    nc.gpsimd.tensor_tensor(DS[:, :], first_in, P[:, n % NP, :], ALU.add).then_inc(den_acc, 1)
                elif kind == "stats" and L == 2:
                    wait_x(pool, L, b)
                    if b == 1:
                        pool.wait_ge(kvn_done, 1)
                        wait_tile(pool, ("v", 3, 0))
                    xv = X[b][:, :].rearrange("c (m two) -> c m two", two=2)
                    nc.gpsimd.tensor_tensor(KP, xv[:, :, 0], xv[:, :, 1], ALU.add).then_inc(pool_chain, 1)
                    links += 1
                    pool.wait_ge(pool_chain, links)
                    kv2 = KP.rearrange("c (i two j) -> c i two j", two=2, j=16)
                    kvo = KV[:, :].rearrange("c (i j) -> c i j", j=16)
                    nc.gpsimd.tensor_tensor(kvo, kv2[:, :, 0, :], kv2[:, :, 1, :], ALU.add).then_inc(pool_chain, 1)
                    links += 1
                    pool.wait_ge(pool_chain, links)
                    nc.gpsimd.tensor_scalar(KV[:, :], KV[:, :], 0.25, None, ALU.mult).then_inc(pooled, 1)

        @block.scalar
        def _(act):
            for s in plan:
                kind, L, b = s[0], s[1], s[2] if len(s) > 2 else None
                if kind == "fold":
                    wait_tile(act, s)
                    nc.scalar.activation(w3vo[:, :], slot(s)[:, 0:C], ACT.Identity)
                    nc.scalar.activation(b3eff[:, :], slot(s)[:, HALF:HALF + 1], ACT.Identity,
                                         bias=w("b3o")).then_inc(read_act, 1)
                elif kind in ("qk", "q", "k"):
                    wait_tile(act, s)
                    if kind == "qk":
                        wait_stage_free(act, s)
                        nc.scalar.activation(Hs[0:32, :], slot(s)[0:32, :], ACT.Identity,
                                             bias=w(f"b{L}qk")[0:32, :]).then_inc(hi_done, 1)
                    elif L == 2 and kind == "q":
                        wait_stage_free(act, s)
                        nc.scalar.activation(Hs[:, :], slot(s), ACT.Identity).then_inc(hi_done, 1)
                    elif L == 2:
                        if b == 1:
                            act.wait_ge(stacks_in[0], stacks_count(2, 0) - 0)
                        nc.scalar.activation(HK[:, :], slot(s)[:, 0:NKV], ACT.Identity).then_inc(hi_done, 1)
                    else:
                        wait_ops_free(act, L, b)
                        k0 = 0 if kind == "q" else 8
                        nc.scalar.activation(ST[b][:, k0, :], slot(s), ACT.Identity,
                                             bias=w("b3" + kind)).then_inc(hi_done, 1)
                elif kind == "v" and L > 0:
                    wait_tile(act, s)
                    if L == 2:
                        act.wait_ge(cleared_pool, 20)
                        v = slot(s)[:, 0:2 * C].rearrange("p (r g h d) -> p r g h d", r=2, g=2, h=HG)
                        nc.scalar.activation(V2[b][:, :, 0, :, 0:D2], v[:, 0], ACT.Identity)
                        nc.scalar.activation(V2[b][:, :, 1, :, 0:D2], v[:, 1], ACT.Identity).then_inc(read_act, 1)
                    else:
                        if L == 3:
                            act.wait_ge(pv_done, pv_done_at[("B", 1, b, 0, 7)])
                        nc.scalar.activation(V13[b][:, :, :].rearrange("p t c -> p (t c)"), slot(s), ACT.Identity,
                                             scale=w("gam1") if L == 1 else 1.0).then_inc(read_act, 1)
                elif kind == "top":
                    wait_tile(act, s)
                    i = top_no[s] % 2
                    if top_no[s] >= 2:
                        p = list(top_no)[top_no[s] - 2]
                        act.wait_ge(maxrows_in[p[2]], max_count(*p[1:]))
                    rows = 64 if L == 2 else 16
                    nc.scalar.activation(ZR[0:rows, i, :], slot(s)[0:rows, 0:128], ACT.Identity).then_inc(read_act, 1)
                elif kind == "B":
                    n = b_no[s]
                    wait_tile(act, s)
                    if n >= NP:
                        p = b_order[n - NP]
                        act.wait_ge(pv_done, pv_done_at[p])
                        q = p if p in den_no else p[:4] + (1,)
                        if q in den_no:
                            act.wait_ge(den_acc, den_no[q])
                    nc.scalar.activation(P[:, n % NP, :], slot(s), ACT.Exp, scale=SCALE[L]).then_inc(read_act, 1)
                elif kind == "out":
                    u = s[1:]
                    act.wait_ge(pv_done, pv_done_at[("B", *u, 7)])
                    before = [v for v in list(out_no)[:out_no[s]] if o_tile[v[1:]] == o_tile[u]]
                    if before:
                        pl, pb, pg = before[-1][1:]
                        if pl == 0:
                            wait_tile(act, ("y", 0, pb))
                        elif pl == 2:
                            wait_tile(act, ("y", 2, pb))
                        else:
                            wait_read(act, ("bcast", pl, pb, pg))
                    nc.scalar.activation(O[o_tile[u]][:, :], acc[:, :], ACT.Identity).then_inc(acc_out, 1)
                elif kind == "y" and L == 0:
                    wait_tile(act, s)
                    if x_upd_before(s):
                        act.wait_ge(x_upd, x_upd_before(s))
                    nc.scalar.activation(T[:, :], slot(s), ACT.Identity).then_inc(read_act, 1)
                elif kind == "rows":
                    wait_tile(act, s)
                    p = previous("bcast", s)
                    if p:
                        wait_tile(act, p)
                    nc.scalar.activation(RT[:, :], slot(s)[:, 0:128], ACT.Identity).then_inc(read_act, 1)
                elif kind == "norm":
                    act.wait_ge(coef_done, norm_no[s] + 1)
                    p = previous("q", s)
                    if p:
                        wait_tile(act, ("k", 3, p[2]) if p[1] == 3 else p)
                        if p[1] == 3:
                            wait_tile(act, ("v", 3, p[2]))
                    nc.scalar.activation(XN[:, :], X[b][:, :], ACT.Identity, scale=ab[:, 0, 0:1],
                                         bias=ab[:, 0, 1:2]).then_inc(xn_done, 1)

        @block.vector
        def _(dve):
            links = [0]

            def link(ins):
                links[0] += 1
                ins.then_inc(dve_chain, 1)
                dve.wait_ge(dve_chain, links[0])

            for s0 in (0, 4):
                nc.vector.memset(ST[0][:, s0:s0 + 2, :].bitcast(F32), 0.0).then_inc(cleared_dve, 1)
            dve.wait_ge(w1_in, 16)
            link(nc.vector.tensor_tensor(w("w0o").rearrange("p (h e) -> p h e", h=H0),
                                         w("w0o").rearrange("p (h e) -> p h e", h=H0),
                                         w("gam0").unsqueeze(2).broadcast_to([128, H0, 32]), ALU.mult))
            nc.vector.tensor_tensor(gb0[:, :], w("gam0c"), w("b0o"), ALU.mult).then_inc(consts_ready, 1)
            late = False
            for s in plan:
                kind, L, b = s[0], s[1], s[2] if len(s) > 2 else None
                if kind == "qk" and L == 1 and not late:
                    late = True
                    dve.wait_ge(w2_in, 16)
                    nc.vector.tensor_tensor(gb1[:, :], w("gam1"), w("b1v"), ALU.mult).then_inc(consts_ready, 1)
                if kind in ("qk", "q", "k"):
                    dve.wait_ge(hi_done, hi_no[s] + 1)
                    wait_tile(dve, s)
                    if kind == "qk":
                        wait_stage_free(dve, s)
                        nc.vector.scalar_tensor_tensor(
                            out=Ls[0:32, :], in0=slot(s)[0:32, :], scalar=w(f"b{L}qk")[0:32, :],
                            in1=Hs[0:32, :].bitcast(F32), op0=ALU.add, op1=ALU.subtract).then_inc(read_dve, 1)
                    elif L == 2 and kind == "q":
                        wait_stage_free(dve, s)
                        nc.vector.tensor_tensor(Ls[:, :], slot(s), Hs[:, :].bitcast(F32), ALU.subtract).then_inc(read_dve, 1)
                    elif L == 2:
                        if b == 1:
                            dve.wait_ge(stacks_in[0], stacks_count(2, 0))
                        nc.vector.tensor_tensor(LK[:, :], slot(s)[:, 0:NKV], HK[:, :].bitcast(F32),
                                                ALU.subtract).then_inc(read_dve, 1)
                    else:
                        k0 = 0 if kind == "q" else 8
                        wait_ops_free(dve, L, b)
                        nc.vector.scalar_tensor_tensor(
                            out=ST[b][:, k0 + 1, :], in0=slot(s), scalar=w("b3" + kind),
                            in1=ST[b][:, k0, :].bitcast(F32), op0=ALU.add, op1=ALU.subtract).then_inc(read_dve, 1)
                elif kind == "v" and L == 0:
                    wait_tile(dve, s)
                    dve.wait_ge(cleared_pool, 6 if b == 0 else 15)
                    nc.vector.tensor_tensor(
                        V0[b][:, :, :, 0:D0],
                        slot(s)[:, 0:NT * 16].rearrange("p (t h d) -> p h t d", t=NT, h=H0),
                        w("b0v").rearrange("p (h d) -> p h d", h=H0).unsqueeze(2).broadcast_to([128, H0, NT, D0]),
                        ALU.add).then_inc(read_dve, 1)
                elif kind == "A":
                    g, t = s[3], s[4]
                    u = split_no[("split", *s[1:4])]
                    wait_tile(dve, s)
                    if t == 0 and u >= 2:
                        dve.wait_ge(split_done, u - 1)
                    if L == 2:
                        nc.vector.tensor_reduce(out=NM[:, u % 2, 4 * t:4 * t + 4],
                                                in_=slot(s).rearrange("p (k r) -> p k r", k=4),
                                                op=ALU.max, axis=AX.X, negate=True).then_inc(read_dve, 1)
                    else:
                        nc.vector.tensor_reduce(out=NM[:, u % 2, t:t + 1], in_=slot(s), op=ALU.max, axis=AX.X,
                                                negate=True).then_inc(read_dve, 1)
                elif kind == "split":
                    u = split_no[s]
                    nk = 32 if L == 2 else 8
                    wait_read(dve, ("A", *s[1:4], 7))
                    if u >= 2:
                        wait_tile(dve, ("top", *list(split_no)[u - 2][1:]))
                    Z = ZT[:, u % 2, :, :].rearrange("p a k -> p (a k)")
                    link(nc.vector.tensor_copy(Z[:, 0:nk].bitcast(F32R), NM[:, u % 2, 0:nk]))
                    nc.vector.tensor_tensor(Z[:, nk:2 * nk], NM[:, u % 2, 0:nk], Z[:, 0:nk],
                                            ALU.subtract).then_inc(split_done, 1)
                elif kind == "den":
                    wait_tile(dve, s)
                    dve.wait_ge(cleared_pool, 14)
                    p = previous("rows", s)
                    if p:
                        wait_tile(dve, p)
                    nc.vector.reciprocal(RC[:, 0:32], slot(s)[:, 0:32]).then_inc(read_dve, 1)
                elif kind == "bcast":
                    g = s[3]
                    o = O[o_tile[(L, b, g)]]
                    wait_tile(dve, s)
                    if L == 0:
                        wait_read(dve, ("y", 0, b))
                        nc.vector.tensor_tensor(T[:, :], T[:, :], slot(s), ALU.mult).then_inc(read_dve, 1)
                        wait_read(dve, s)
                        dve.wait_ge(consts_ready, 1)
                        nc.vector.scalar_tensor_tensor(out=X[b][:, :], in0=T[:, :], scalar=gb0[:, 0:1], in1=X[b][:, :],
                                                       op0=ALU.add, op1=ALU.add).then_inc(x_upd, 1)
                    elif L == 2:
                        dve.wait_ge(acc_out, out_no[("out", L, b, g)] + 1)
                        nc.vector.tensor_tensor(o[:, :], o[:, :], slot(s), ALU.mult).then_inc(read_dve, 1)
                    else:
                        dve.wait_ge(acc_out, out_no[("out", L, b, g)] + 1)
                        if x_upd_before(s):
                            dve.wait_ge(x_upd, x_upd_before(s))
                        nc.vector.tensor_tensor(T[:, :], o[:, :], slot(s), ALU.mult).then_inc(read_dve, 1)
                        wait_read(dve, s)
                        if L == 1:
                            dve.wait_ge(consts_ready, 2)
                        else:
                            wait_read(dve, ("fold", 3))
                        nc.vector.scalar_tensor_tensor(out=X[b][:, :], in0=T[:, :],
                                                       scalar=gb1[:, 0:1] if L == 1 else b3eff[:, 0:1], in1=X[b][:, :],
                                                       op0=ALU.add, op1=ALU.add).then_inc(x_upd, 1)
                elif kind == "y" and L == 2:
                    wait_tile(dve, s)
                    nc.vector.tensor_tensor(X[b][:, :], slot(s), X[b][:, :], ALU.add).then_inc(read_dve, 1)
                elif kind == "stats":
                    ni = 2 if L == 2 else 1
                    wait_x(dve, L, b)
                    nc.vector.bn_stats(bn[:, 0, :], X[b][:, 0:HALF])
                    link(nc.vector.bn_stats(bn[:, 1, :], X[b][:, HALF:N]))
                    link(nc.vector.bn_aggr(mv[:, 0, :], bn[:, 0:2, :]))
                    if L == 2:
                        dve.wait_ge(pooled, b + 1)
                        link(nc.vector.bn_stats(bn[:, 2, :], KV[:, :]))
                        link(nc.vector.bn_aggr(mv[:, 1, :], bn[:, 2:3, :]))
                    link(nc.vector.tensor_tensor(nt[:, 0, 0:ni], mv[:, 0:ni, 0], mv[:, 0:ni, 0], ALU.mult))
                    nc.vector.tensor_tensor(mv[:, 0:ni, 1], mv[:, 0:ni, 1], nt[:, 0, 0:ni], ALU.add).then_inc(stats_done, 1)
                elif kind == "norm":
                    ni = 2 if L == 2 else 1
                    wait_tile(dve, s)
                    nc.vector.tensor_copy(gs[:, 0:ni, :], slot(s)[:, 0:2 * ni].rearrange("p (i k) -> p i k", k=2)).then_inc(read_dve, 1)
                    wait_read(dve, s)
                    mean, ex2 = gs[:, 0:ni, 0], gs[:, 0:ni, 1]
                    v, y, a = nt[:, 1, 0:ni], nt[:, 2, 0:ni], nt[:, 3, 0:ni]
                    link(nc.vector.tensor_tensor(a, mean, mean, ALU.mult))
                    link(nc.vector.tensor_tensor(v, ex2, a, ALU.subtract))
                    link(nc.vector.tensor_scalar(v, v, 0.0, EPS, ALU.max, ALU.add))
                    link(nc.vector.tensor_scalar(a.bitcast(I32), v.bitcast(I32), 1, None, ALU.arith_shift_right))
                    link(nc.vector.tensor_scalar(y.bitcast(I32), a.bitcast(I32), -1.0, float(RSQRT_SEED), ALU.mult, ALU.add))
                    for _ in range(4):
                        link(nc.vector.tensor_tensor(a, y, y, ALU.mult))
                        link(nc.vector.tensor_tensor(a, a, v, ALU.mult))
                        link(nc.vector.tensor_scalar(a, a, -0.5, 1.5, ALU.mult, ALU.add))
                        link(nc.vector.tensor_tensor(y, y, a, ALU.mult))
                    gn = w(f"gn{L}").rearrange("p (i k) -> p i k", k=2)
                    if norm_no[s]:
                        dve.wait_ge(xn_done, norm_no[s])
                    link(nc.vector.tensor_tensor(ab[:, 0:ni, 0], y, gn[:, 0:ni, 0], ALU.mult))
                    link(nc.vector.tensor_tensor(a, mean, ab[:, 0:ni, 0], ALU.mult))
                    nc.vector.tensor_tensor(ab[:, 0:ni, 1], gn[:, 0:ni, 1], a, ALU.subtract).then_inc(coef_done, 1)
                    if L == 2:
                        dve.wait_ge(coef_done, norm_no[s] + 1)
                        if b == 1:
                            wait_tile(dve, ("v", 2, 0))
                        nc.vector.tensor_scalar(KVN[:, :], KV[:, :], ab[:, 1, 0:1], ab[:, 1, 1:2],
                                                ALU.mult, ALU.add).then_inc(kvn_done, 1)

        @block.tensor
        def _(pe):
            halves = (slice(0, HALF), slice(HALF, N))

            def full(s, mm):
                mm.then_inc(tile_full, 1)

            for s in plan:
                kind, L, b = s[0], s[1], s[2] if len(s) > 2 else None
                if s in job and job[s] >= RING:
                    wait_read(pe, jobs[job[s] - RING])
                if kind == "fold":
                    pe.wait_ge(w2_in, 16)
                    nc.tensor.matmul(slot(s)[:, 0:C], w("w3v"), w("w3o"), start=True, stop=True)
                    full(s, nc.tensor.matmul(slot(s)[:, HALF:HALF + 1], w("w3o"), w("b3v"), start=True, stop=True))
                elif kind in ("qk", "q"):
                    if L in (0, 1):
                        if L == 0:
                            pe.wait_ge(w1_in, 16)
                        wait_x(pe, L, b)
                        for h in halves:
                            mm = nc.tensor.matmul(slot(s)[0:32, h], w(f"w{L}qk"), X[b][:, h], start=True, stop=True)
                    else:
                        pe.wait_ge(xn_done, norm_no[("norm", L, b)] + 1)
                        for h in halves:
                            mm = nc.tensor.matmul(slot(s)[:, h], w(f"w{L}q"), XN[:, h], start=True, stop=True)
                    full(s, mm)
                elif kind == "k":
                    if L == 2:
                        pe.wait_ge(kvn_done, b + 1)
                        full(s, nc.tensor.matmul(slot(s)[:, 0:NKV], w("w2k"), KVN[:, :], start=True, stop=True))
                    else:
                        for h in halves:
                            mm = nc.tensor.matmul(slot(s)[:, h], w("w3k"), XN[:, h], start=True, stop=True)
                        full(s, mm)
                elif kind == "v":
                    src, wv, width, tiles = {0: (X[b], w("w0v"), 16, NT), 1: (X[b], w("w1v"), C, NT),
                                             2: (KVN, w("w2v"), C, 2), 3: (XN, w3vo[:, :], C, NT)}[L]
                    if L == 3:
                        wait_read(pe, ("fold", 3))
                    for t in range(tiles):
                        mm = nc.tensor.matmul(slot(s)[:, width * t:width * (t + 1)], src[:, 128 * t:128 * (t + 1)], wv,
                                              start=True, stop=True)
                    full(s, mm)
                elif kind == "A":
                    g, t = s[3], s[4]
                    if t == 0:
                        pe.wait_ge(stacks_in[b], stacks_count(L, b))
                        if L == 2:
                            pe.wait_ge(cleared_pool, 20)
                    if L == 3:
                        wait_read(pe, ("q", 3, b))
                        wait_read(pe, ("k", 3, b))
                        for h in halves:
                            mm = nc.tensor.matmul(slot(s)[:, h], ST[b][:, 0, 128 * t:128 * (t + 1)], ST[b][:, 8, h],
                                                  start=True, stop=True)
                    elif L == 2:
                        head = HG * g + t // 2
                        k = ST[b][0:KROWS, 8:10, :].rearrange("p s n -> p (s n)")[:, NKV * head:NKV * (head + 1)]
                        for i in range(4):
                            kt = 4 * (t % 2) + i
                            mm = nc.tensor.matmul(slot(s)[:, NKV * i:NKV * (i + 1)],
                                                  ST[b][0:KROWS, head, 128 * kt:128 * (kt + 1)], k,
                                                  start=True, stop=True)
                    else:
                        ks, rs = (g, 4 + g) if L == 0 else (0, 4)
                        for h in halves:
                            mm = nc.tensor.matmul(slot(s)[:, h], ST[b][0:KROWS, ks, 128 * t:128 * (t + 1)],
                                                  ST[b][0:KROWS, rs, h], start=True, stop=True)
                    full(s, mm)
                elif kind == "top":
                    u = split_no[("split", *s[1:])]
                    nk = 32 if L == 2 else 8
                    pe.wait_ge(split_done, u + 1)
                    full(s, nc.tensor.transpose(slot(s)[0:2 * nk, 0:128],
                                                ZT[:, u % 2, :, :].rearrange("p a k -> p (a k)")[:, 0:2 * nk], w("ident")))
                elif kind == "B":
                    g, t = s[3], s[4]
                    if t == 0:
                        pe.wait_ge(maxrows_in[b], max_count(L, b, g))
                    if L == 3:
                        if t == 0:
                            pe.wait_ge(cleared_pool, 20)
                        tile = slice(128 * t, 128 * (t + 1))
                        for h in halves:
                            nc.tensor.matmul(slot(s)[:, h], pick[:, :], ST[b][0:KROWS, 2, h], start=True, stop=False)
                        for i, (r, k) in enumerate(((8, 0), (8, 1), (9, 0), (9, 1))):
                            for h in halves:
                                mm = nc.tensor.matmul(slot(s)[:, h], ST[b][:, r, tile], ST[b][:, k, h],
                                                      start=False, stop=i == 3)
                    else:
                        if L == 2:
                            head, rt = HG * g + t % 4, t // 4
                            ks = head
                            red = ST[b][0:KROWS, 8:10, :].rearrange("p s n -> p (s n)")[
                                :, NKV * head + 128 * rt:NKV * head + 128 * (rt + 1)]
                        else:
                            ks = g if L == 0 else 0
                            red = ST[b][0:KROWS, 4 + ks, 128 * t:128 * (t + 1)]
                        for h in halves:
                            mm = nc.tensor.matmul(slot(s)[:, h], red, ST[b][0:KROWS, ks, h], start=True, stop=True)
                    full(s, mm)
                elif kind in ("PV4", "PV1"):
                    g, t0 = s[3], s[4]
                    if t0 == 0:
                        if out_no[("out", L, b, g)]:
                            pe.wait_ge(acc_out, out_no[("out", L, b, g)])
                        if L == 0:
                            wait_read(pe, ("v", 0, b))
                        else:
                            wait_read(pe, ("v", L, b))
                    if kind == "PV4":
                        tiles = [("B", L, b, g, 4 * t0 + j) for j in range(4)]
                        wait_read(pe, tiles[3])
                        for h in halves:
                            for j, q in enumerate(tiles):
                                lhs = V0[b][:, g, 4 * t0 + j, :] if L == 0 else V2[b][:, g, t0, j, :]
                                mm = nc.tensor.matmul(acc[32 * j:32 * j + 32, h], lhs, P[:, b_no[q] % NP, h],
                                                      start=t0 == 0, stop=t0 == 1)
                                if h.start:
                                    mm.then_inc(pv_done, 1)
                    else:
                        q = ("B", L, b, g, t0)
                        wait_read(pe, q)
                        for h in halves:
                            mm = nc.tensor.matmul(acc[:, h], V13[b][:, t0, :], P[:, b_no[q] % NP, h],
                                                  start=t0 == 0, stop=t0 == 7)
                        mm.then_inc(pv_done, 1)
                elif kind == "den":
                    g = s[3]
                    if L in (0, 2):
                        pe.wait_ge(acc_out, out_no[("out", L, b, g)] + 1)
                    else:
                        pe.wait_ge(den_acc, den_no[("B", L, b, g, 7)])
                    for t in range(NT):
                        tile = slice(128 * t, 128 * (t + 1))
                        if L == 0:
                            for h in range(H0):
                                mm = nc.tensor.matmul(slot(s)[:, 4 * t + h:4 * t + h + 1], O[h][:, tile], w("x0den"),
                                                      start=True, stop=True)
                        else:
                            src, sel = (O[o_tile[(L, b, g)]], w("sel2")) if L == 2 else (DS, w("ones4"))
                            mm = nc.tensor.matmul(slot(s)[:, 4 * t:4 * t + 4], src[:, tile], sel, start=True, stop=True)
                    full(s, mm)
                elif kind == "rows":
                    wait_read(pe, ("den", *s[1:]))
                    full(s, nc.tensor.transpose(slot(s)[:, 0:128], RC[:, :], w("ident")))
                elif kind == "bcast":
                    wait_read(pe, ("rows", *s[1:]))
                    sel = w("sel").rearrange("p (t c) -> p t c", t=NT)
                    for t in range(NT):
                        mm = nc.tensor.matmul(slot(s)[:, 128 * t:128 * (t + 1)], sel[:, t, :], RT[:, :],
                                              start=True, stop=True)
                    full(s, mm)
                elif kind == "y" and L == 0:
                    pe.wait_ge(consts_ready, 1)
                    pe.wait_ge(acc_out, out_no[("out", 0, b, 3)] + 1)
                    for h in halves:
                        for i in range(H0):
                            mm = nc.tensor.matmul(slot(s)[32 * i:32 * i + 32, h], w("w0o")[:, 32 * i:32 * i + 32],
                                                  O[i][:, h], start=True, stop=True)
                    full(s, mm)
                elif kind == "y":
                    wait_read(pe, ("bcast", 2, b, 1))
                    for h in halves:
                        for g in range(2):
                            mm = nc.tensor.matmul(slot(s)[:, h], w("w2p")[:, 128 * g:128 * (g + 1)],
                                                  O[o_tile[(2, b, g)]][:, h], start=g == 0, stop=g == 1)
                    full(s, mm)
                elif kind == "norm":
                    pe.wait_ge(stats_done, norm_no[s] + 1)
                    ni = 2 if L == 2 else 1
                    full(s, nc.tensor.matmul(slot(s)[:, 0:2 * ni], w("avg16" if L == 2 else "avg4"),
                                             mv[:, 0:ni, :].rearrange("p i k -> p (i k)"), start=True, stop=True))


def pack(layout, parts):
    import numpy as np

    at, n = columns(layout)
    out = np.zeros((128, n), np.float32)
    for name, a in parts.items():
        out[:a.shape[0], at[name][0]:at[name][0] + a.shape[1]] = a
    return out


def kernel(**inputs):
    import numpy as np
    import concourse.bacc as bacc
    from concourse.bass_utils import run_bass_kernel_spmd

    a = {k: np.asarray(v) for k, v in inputs.items()}

    def col(v):
        return v.reshape(-1, 1)

    def dh(wt, h, d):
        return wt.reshape(h, d, C).transpose(1, 0, 2).reshape(h * d, C)

    def dhb(bias, h, d):
        return bias.reshape(h, d).transpose(1, 0).reshape(-1)

    w0qk = np.concatenate([dh(a["L0_conv_Wk"], H0, D0), dh(a["L0_conv_Wq"], H0, D0)]).T
    b0qk = col(np.concatenate([dhb(a["L0_conv_bk"], H0, D0), dhb(a["L0_conv_bq"], H0, D0)]))
    w0o = np.zeros((4, 32, H0, 32), np.float32)
    for j in range(4):
        w0o[j, 0:D0] = a["L0_conv_Wo"].transpose(2, 0, 1)
    x0den = np.zeros((4, 32, 1), np.float32)
    x0den[:, D0] = 1
    gam0 = a["L0_conv_gamma"]
    first = pack(FIRST, {
        "w0qk": w0qk, "b0qk": b0qk,
        "w0v": a["L0_conv_Wv"].reshape(16, C).T,
        "b0v": np.broadcast_to(a["L0_conv_bv"].reshape(1, 16), (128, 16)),
        "x0den": x0den.reshape(128, 1),
        "gam0": np.broadcast_to(gam0.reshape(1, 4), (128, 4)),
        "gam0c": col(np.repeat(gam0, 32)), "b0o": col(a["L0_conv_bo"]),
        "w0o": w0o.reshape(128, 128), "ident": np.eye(128, dtype=np.float32)})
    sel = np.zeros((NT, 4, NT, 4, 32), np.float32)
    for t in range(NT):
        for h in range(4):
            sel[t, h, t, h] = 1
    selp = np.zeros((128, 1024), np.float32)
    selp[0:32] = sel.reshape(32, 1024)
    w2p = np.zeros((HG, 32, 2, C), np.float32)
    w2p[:, 0:D2] = a["L2_conv_wproj"].T.reshape(2, HG, D2, C).transpose(1, 2, 0, 3)
    sel2 = np.zeros((HG, 32, HG), np.float32)
    for h in range(HG):
        sel2[h, D2, h] = 1
    qkv, qkvb = a["L3_conv_qkv_w"], a["L3_conv_qkv_b"]

    def blocks(n):
        m = np.zeros((C // n, n, C // n, n), np.float32)
        for i in range(C // n):
            m[i, :, i, :] = 1.0 / n
        return m.reshape(C, C)

    rest = pack(REST, {
        "sel": selp,
        "w1qk": np.concatenate([a["L1_conv_wq"], a["L1_conv_wk"]]).T,
        "b1qk": col(np.concatenate([a["L1_conv_bq"], a["L1_conv_bk"]])),
        "w1v": a["L1_conv_wv"].T, "b1v": col(a["L1_conv_bv"]),
        "gam1": np.broadcast_to(a["L1_conv_gamma"].reshape(1, 1), (128, 1)),
        "w2q": dh(a["L2_conv_wq"], H2, D2).T, "w2k": dh(a["L2_conv_wk"], H2, D2).T, "w2v": a["L2_conv_wv"].T,
        "w2p": w2p.reshape(128, 256),
        "gn2": np.stack([a["L2_conv_gnq_w"], a["L2_conv_gnq_b"], a["L2_conv_gnk_w"], a["L2_conv_gnk_b"]], 1),
        "avg16": blocks(16), "sel2": sel2.reshape(128, 4), "ones4": np.ones((128, 4), np.float32),
        "w3q": qkv[0:C].T, "w3k": qkv[C:2 * C].T, "w3v": qkv[2 * C:], "w3o": a["L3_conv_out_w"].T,
        "b3q": col(qkvb[0:C]), "b3k": col(qkvb[C:2 * C]), "b3v": col(qkvb[2 * C:]), "b3o": col(a["L3_conv_out_b"]),
        "gn3": np.stack([a["L3_conv_gn_w"], a["L3_conv_gn_b"]], 1), "avg4": blocks(4)})
    x = np.ascontiguousarray(a["x"]).reshape(B, C, N)

    nc = bacc.Bacc("TRN2", target_bir_lowering=False, num_devices=1)
    arrays = {"x": x, "w_first": first, "w_rest": rest}
    args = [nc.dram_tensor(n, v.shape, F32, kind="ExternalInput").ap() for n, v in arrays.items()]
    out = nc.dram_tensor("y", (B, C, N), F32, kind="ExternalOutput").ap()
    attention_layers(nc, *args, out)
    r = run_bass_kernel_spmd(nc, [arrays], core_ids=[0])
    return r.results[0]["y"].reshape(B, C, 32, 32)
```

```python
from contextlib import ExitStack

import concourse.bass as bass
from concourse import mybir

F32 = mybir.dt.float32
F32R = mybir.dt.float32r
I32 = mybir.dt.int32
ALU = mybir.AluOpType
ACT = mybir.ActivationFunctionType
AX = mybir.AxisListType

B, C, N = 2, 128, 1024
NT = N // 128
HALF = 512
NKV = 256
H0, D0 = 4, 4
D1 = 16
H2, D2 = 8, 16
HG = 4
MAXROW = 64
KROWS = 96
RING = 3
NP = 8
O_TILES = 5
EPS = 1e-5
SCALE = {0: 1.0, 1: 1.0, 2: float(D2) ** -0.5, 3: float(C) ** -0.5}
RSQRT_SEED = 0x5F3759DF

FIRST = [("w0qk", 128), ("b0qk", 1), ("lo_sign", 1), ("w0v", 16), ("b0v", 16), ("gam0", 4), ("gam0c", 1),
         ("b0o", 1), ("w0o", 128), ("ident", 128)]
REST = [("den0", 32), ("pick4", 4), ("w1qk", 128), ("b1qk", 1), ("w1v", 128), ("b1v", 1), ("gam1", 1),
        ("w2q", 128), ("w2k", 128), ("w2v", 128), ("w2p", 256), ("gn2", 4), ("avg16", 128),
        ("sel2", 4), ("ones4", 4), ("w3q", 128), ("w3k", 128), ("w3v", 128), ("w3o", 128), ("b3q", 1),
        ("b3k", 1), ("b3v", 1), ("b3o", 1), ("gn3", 2), ("avg4", 128)]


def columns(layout):
    at, out = 0, {}
    for name, width in layout:
        out[name] = (at, width)
        at += width
    return out, at


UNITS = [(0, 0, 0), (0, 0, 1), (0, 0, 2), (0, 0, 3), (0, 1, 0), (0, 1, 1), (1, 0, 0), (0, 1, 2), (0, 1, 3),
         (2, 0, 0), (2, 0, 1), (1, 1, 0), (3, 0, 0), (2, 1, 0), (2, 1, 1), (3, 1, 0)]
GROUPS = {0: 4, 1: 1, 2: 2, 3: 1}
ORDER = (
    "NNAAAAVAAAAAATAAA"
    "BABBABABAAABPTABABAAAP"
    "BABBBABBVAAAAPPTABAABAA"
    "BAAPAPBBTBBAVBPABABA"
    "BABABPPBBBBAPBAAAPATAAPEEA"
    "BBEAAEEBBBBBNTBPPA"
    "BBAAABABABABAABVPATAAAPB"
    "BBAAAABPAAAPPAAAPBATBPBABBPAP"
    "BPPABPPEEBEBTBNBNPNBB"
    "BBBPNBBPBBBPAAAAAPPAAAAETVAEE"
    "BEABABABEBBBAANPBAAVAAATPAAP"
    "BBABBAABAABETBBEPPPEE"
    "BEBBEPENBBPNPPBPNNBBPAAAPAPPAAEAAEAETV"
    "BNNBBNBNPBPBPVAAAPAABAPAAABATPAAAPA"
    "BBPBABABABPAETBBPE"
    "BBBBPPBBEEBBPEPEPEEEENNNNVAAAAAAAAAT"
    "BBBBBPPPPBPPBBPPPEEE"
)


def prologue(L, b):
    if L in (0, 1):
        return [("qk", L, b), ("v", L, b)]
    return [("stats", L, b), ("norm", L, b), ("q", L, b), ("k", L, b), ("v", L, b)]


def epilogue(L, b, g):
    if L == 0:
        return [("dsum", L, b), ("y", L, b), ("den", L, b, g), ("rows", L, b, g), ("bcast", L, b, g)] if g == 3 else []
    if L == 2:
        return [("den", L, b, g), ("rows", L, b, g), ("bcast", L, b, g)] + ([("y", L, b)] if g == 1 else [])
    return [("den", L, b, g), ("rows", L, b, g), ("bcast", L, b, g)]


def last_step(L, b):
    return ("y", L, b) if L == 2 else ("bcast", L, b, GROUPS[L] - 1)


def build_plan():
    steps = {c: [] for c in "ATBPENV"}
    for L, b, g in UNITS:
        if g == 0:
            for s in prologue(L, b):
                steps["V" if s[0] == "v" else "N"].append(s)
        steps["A"] += [("A", L, b, g, t) for t in range(8)] + [("split", L, b, g)]
        steps["T"] += [("top", L, b, g)]
        steps["B"] += [("B", L, b, g, t) for t in range(8)]
        steps["P"] += [("PV4", L, b, g, i) for i in range(2)] if L in (0, 2) else [
            ("PV1", L, b, g, t) for t in range(8)]
        steps["P"] += [("out", L, b, g)]
        steps["E"] += epilogue(L, b, g)
    steps["V"].insert(2, ("fold", 3))
    following = {c: iter(s) for c, s in steps.items()}
    return [next(following[c]) for c in ORDER]


def attention_layers(nc, x, first, rest, sel, out):
    plan = build_plan()
    assert len(set(plan)) == len(plan)

    def last_reader(s):
        kind, L = s[0], s[1]
        if kind in ("A", "norm", "den", "bcast", "qk", "q", "k") or (kind, L) in (("v", 0), ("y", 2)):
            return "dve"
        if kind in ("B", "top", "rows", "fold", "dsum") or (kind, L) in (("v", 1), ("v", 2), ("v", 3), ("y", 0)):
            return "act"
        return None

    jobs = [s for s in plan if last_reader(s)]
    job = {s: n for n, s in enumerate(jobs)}
    read = {}
    for who in ("dve", "act"):
        for n, s in enumerate([s for s in jobs if last_reader(s) == who]):
            read[s] = n + 1

    def number(kinds, layers=(0, 1, 2, 3)):
        return {s: n for n, s in enumerate([s for s in plan if s[0] in kinds and s[1] in layers])}

    b_no = number(("B",))
    b_order = list(b_no)
    hi_no = number(("qk", "q", "k"))
    stage = [s for s in plan if s[0] in ("qk", "q") and s[1] < 3]
    top_no = number(("top",))
    split_no = number(("split",))
    out_no = number(("out",))
    x_no = {}
    for s in plan:
        if s[0] == "bcast" and s[1] != 2 and s == last_step(s[1], s[2]):
            x_no[(s[1], s[2])] = len(x_no) + 1
    recip_no = number(("den",))
    den_ops = [s for s in plan if s[0] == "PV1" and s[4] > 0]
    den_no = {s: n + 1 for n, s in enumerate(den_ops)}
    o_last = {(L, b, g): ("y", L, b) if L in (0, 2) else ("bcast", L, b, g) for L, b, g in UNITS}
    o_tile, o_before, free, held = {}, {}, [(i, None) for i in range(O_TILES)], []
    for s in plan:
        if s[0] == "out":
            tile, before = free.pop(0)
            o_tile[s[1:]], o_before[s[1:]] = tile, before
            held.append(s[1:])
        for u in [u for u in held if o_last[u] == s]:
            held.remove(u)
            free.append((o_tile[u], u))
    pv_done_at = {}
    n = 0
    for s in plan:
        if s[0] == "PV4":
            for t in range(4 * s[4], 4 * s[4] + 4):
                n += 1
                pv_done_at[("B", *s[1:4], t)] = n
        elif s[0] == "PV1":
            n += 1
            pv_done_at[("B", *s[1:4], s[4])] = n

    col1, n1 = columns(FIRST)
    col2, n2 = columns(REST)

    with ExitStack() as ctx:
        def sb(name, shape, dt=F32):
            return ctx.enter_context(nc.sbuf_tensor(name, shape, dt))

        def sem(name):
            return ctx.enter_context(nc.semaphore(name))

        w1 = sb("w1", [128, n1])
        w2 = sb("w2", [128, n2])
        selr = sb("head_rows_to_channels", [128, NT, C], F32R)

        def w(name):
            a, width = (col1 if name in col1 else col2)[name]
            return (w1 if name in col1 else w2)[:, a:a + width]

        X = [sb(f"x{b}", [C, N]) for b in range(B)]
        ST = [sb(f"score_ops{b}", [128, 10, N], F32R) for b in range(B)]
        Hs = sb("stage_hi", [128, N], F32R)
        Ls = sb("stage_lo", [128, N], F32R)
        HK = sb("stage_k_hi", [128, NKV], F32R)
        LK = sb("stage_k_lo", [128, NKV], F32R)
        P = sb("probs", [128, NP, N])
        V0 = [sb(f"v0_{b}", [128, H0, NT, 32]) for b in range(B)]
        V2 = [sb(f"v2_{b}", [128, 2, 2, HG, 32]) for b in range(B)]
        V13 = [sb(f"v13_{b}", [128, NT, C]) for b in range(B)]
        O = [sb(f"attn_out{i}", [128, N]) for i in range(O_TILES)]
        DS = sb("prob_sum", [128, N])
        T = sb("tmp", [128, N])
        XN = sb("x_norm", [C, N])
        KV = sb("kv_pool", [C, NKV])
        KP = XN[:, 0:512]
        KVN = sb("kv_norm", [C, NKV])
        NM = sb("neg_max", [128, 2, 32])
        ZT = sb("max_halves", [128, 2, 2, 32])
        ZR = sb("max_rows", [64, 2, 128])
        RR = sb("recips", [128, 32])
        RC = sb("recip_cols", [128, 128])
        RT = sb("recip_rows", [128, 128], F32R)
        lob = [sb(f"lo_bias{L}", [128, 1]) for L in (0, 1)]
        const = sb("const_rows", [4, N])
        pick = sb("max_picker", [KROWS, 128], F32R)
        w3vo = sb("w3vo", [C, C])
        b3eff = sb("b3eff", [C, 1])
        gb0 = sb("gamma_bo", [C, 1])
        gb1 = sb("gamma_bv", [C, 1])
        bn = sb("bn_parts", [C, 3, 6])
        mv = sb("mean_var", [C, 2, 2])
        gs = sb("group_stats", [C, 2, 2])
        nt = sb("norm_tmp", [C, 6, 2])
        ab = sb("norm_scale_shift", [C, 2, 2])
        eps = sb("eps", [C, 2])

        ps = ctx.enter_context(nc.psum_tensor("products", [128, RING, N], F32))
        acc = ctx.enter_context(nc.psum_tensor("attn_acc", [128, N], F32))

        x_in = [sem(f"x_in{b}") for b in range(B)]
        w1_in, w2_in, sel_in = sem("w1_in"), sem("w2_in"), sem("sel_in")
        cleared_dve, cleared_pool = sem("cleared_dve"), sem("cleared_pool")
        consts_ready, consts_act = sem("consts_ready"), sem("consts_act")
        tile_full = sem("tile_full")
        read_dve, read_act = sem("tile_read_dve"), sem("tile_read_act")
        signs_done = sem("signs_done")
        hi_done = sem("hi_done")
        stacks_in = [sem(f"stacks_in{b}") for b in range(B)]
        split_done = sem("split_done")
        maxrows_in = [sem(f"maxrows_in{b}") for b in range(B)]
        pv_done = sem("pv_done")
        den_acc = sem("den_acc")
        acc_out = sem("acc_out")
        recip_done = sem("recip_done")
        x_upd = sem("x_upd")
        stats_done = sem("stats_done")
        coef_done = sem("coef_done")
        xn_done, kvn_done = sem("xn_done"), sem("kvn_done")
        dve_chain = sem("dve_chain")
        out_done = sem("out_done")

        def slot(s):
            return ps[:, job[s] % RING, :]

        def wait_tile(eng, s):
            eng.wait_ge(tile_full, job[s] + 1)

        def wait_read(eng, s):
            eng.wait_ge(read_dve if last_reader(s) == "dve" else read_act, read[s])

        def wait_x(eng, L, b):
            if L == 0:
                eng.wait_ge(x_in[b], 16)
            elif L == 3:
                wait_read(eng, ("y", 2, b))
            else:
                eng.wait_ge(x_upd, x_no[(L - 1, b)])

        stack_dmas = {0: 3, 1: 3, 2: 9}

        def stacks_count(L, b):
            return 16 * sum(stack_dmas[i] for i in range(min(L, 2) + 1))

        def wait_stage_free(eng, s):
            i = stage.index(s)
            if i:
                p = stage[i - 1]
                eng.wait_ge(stacks_in[p[2]], stacks_count(p[1], p[2]))

        def wait_ops_free(eng, L, b):
            if L == 0:
                eng.wait_ge(cleared_pool, 3 + b)
                eng.wait_ge(cleared_dve, 1)
            else:
                wait_tile(eng, ("B", L - 1, b, GROUPS[L - 1] - 1, 7))

        def max_count(L, b, g):
            order = [s for s in top_no if s[2] == b]
            return 16 * (order.index(("top", L, b, g)) + 1)

        def previous(kind, s):
            found = [p for p in plan[:plan.index(s)] if p[0] == kind]
            return found[-1] if found else None

        def wait_sum_free(eng, s):
            p = [p for p in plan[:plan.index(s)] if p[0] == "den" and p[1] != 2]
            if p:
                wait_tile(eng, p[-1])

        def wait_norm_free(eng, s):
            p = [p for p in plan[:plan.index(s)] if p[:2] in (("q", 2), ("v", 3))]
            if p:
                wait_tile(eng, p[-1])

        def x_upd_before(s):
            return len([p for p in plan[:plan.index(s)] if p[0] == "bcast" and p[1] != 2])

        norm_no = number(("norm",))

        block = ctx.enter_context(nc.Block())

        @block.sync
        def _(sp):
            sp.dma_start(w1[:, :], first).then_inc(w1_in, 16)
            sp.dma_start(X[0][:, :], x[0]).then_inc(x_in[0], 16)
            sp.dma_start(X[1][:, :], x[1]).then_inc(x_in[1], 16)
            sp.dma_start(w2[:, :], rest).then_inc(w2_in, 16)
            sp.dma_start(T[:, :], sel).then_inc(sel_in, 16)

            def spread(b, rows, r0, slots, parts, kept):
                hi, lo = parts
                d = rows
                for r, src in enumerate((hi, lo, hi, lo) if kept else (hi, hi, lo, lo)):
                    dst = slots(d * r, d * r + d)
                    sp.dma_start(dst, src).then_inc(stacks_in[b], 16)

            for s in plan:
                kind, L, b = s[0], s[1], s[2] if len(s) > 2 else None
                S = ST[b][:, :, :].bitcast(F32) if b is not None else None
                if kind == "qk" or (kind in ("q", "k") and L == 2):
                    wait_ops_free(sp, L, b)
                    mr = S[MAXROW:MAXROW + 2]
                    if kind == "qk" and L == 0:
                        sp.dma_start(mr[:, 4:8, :], const[2:4, :].unsqueeze(1).broadcast_to([2, 4, N])).then_inc(stacks_in[b], 16)
                    elif kind == "qk":
                        sp.dma_start(mr[:, 0, :], const[0:2, :]).then_inc(stacks_in[b], 16)
                    elif kind == "q":
                        sp.dma_start(mr[:, 0:H2, :], const[0:2, :].unsqueeze(1).broadcast_to([2, H2, N])).then_inc(stacks_in[b], 16)
                        sp.wait_ge(hi_done, hi_no[s] + 1)
                    wait_read(sp, s)
                if kind == "qk":
                    rows, heads = (4 * D0, H0) if L == 0 else (4 * D1, 1)
                    for s0, r0 in ((0, 0), (4, 64)):
                        sp.dma_start(S[0:rows, s0:s0 + heads, :], Ls[r0:r0 + 64, :].bitcast(F32)).then_inc(stacks_in[b], 16)
                elif kind == "q" and L == 2:
                    spread(b, D2, 0, lambda a, z: S[a:z, 0:H2, :], (Hs[:, :].bitcast(F32), Ls[:, :].bitcast(F32)), True)
                elif kind == "k" and L == 2:
                    spread(b, D2, 0,
                           lambda a, z: S[a:z, 8:10, :].rearrange("p s n -> p (s n)").rearrange("p (h n) -> p h n", h=H2),
                           (HK[:, :].bitcast(F32), LK[:, :].bitcast(F32)), False)
                elif kind == "top":
                    g = s[3]
                    i = top_no[s] % 2
                    wait_read(sp, s)
                    k0, kn = {0: (g, 1), 1: (0, 1), 2: (HG * g, HG), 3: (2, 1)}[L]
                    sp.dma_start(S[MAXROW:MAXROW + 2, k0:k0 + kn, :], ZR[0:16 * kn, i, :]).then_inc(maxrows_in[b], 16)
                elif kind == "bcast" and L == 3:
                    sp.wait_ge(x_upd, x_no[(3, b)])
                    sp.dma_start(out[b], X[b][:, :]).then_inc(out_done, 16)
            sp.wait_ge(out_done, 16 * B)

        @block.gpsimd
        def _(pool):
            nc.gpsimd.memset(const[:, :], 1.0).then_inc(cleared_pool, 1)
            pool.wait_ge(cleared_pool, 1)
            nc.gpsimd.memset(const[0:2, :], 0.0).then_inc(cleared_pool, 1)
            nc.gpsimd.memset(ST[0][:, 4:8, :].bitcast(F32), 0.0).then_inc(cleared_pool, 1)
            nc.gpsimd.memset(ST[1][:, 0:8, :].bitcast(F32), 0.0).then_inc(cleared_pool, 1)
            for b in range(B):
                nc.gpsimd.memset(V0[b][:, :, :, :], 0.0).then_inc(cleared_pool, 1)
            pool.wait_ge(cleared_pool, 6)
            for b in range(B):
                nc.gpsimd.memset(V0[b][:, :, :, D0:D0 + 1], 1.0).then_inc(cleared_pool, 1)
            for b in range(B):
                nc.gpsimd.memset(ST[b][:, 8:10, :].bitcast(F32), 0.0).then_inc(cleared_pool, 1)
                nc.gpsimd.memset(V2[b][:, :, :, :, :], 0.0).then_inc(cleared_pool, 1)
            nc.gpsimd.memset(pick[:, :].bitcast(F32), 0.0).then_inc(cleared_pool, 1)
            nc.gpsimd.memset(RC[:, :], 0.0).then_inc(cleared_pool, 1)
            pool.wait_ge(cleared_pool, 14)
            for b in range(B):
                nc.gpsimd.memset(V2[b][:, :, :, :, D2:D2 + 1], 1.0).then_inc(cleared_pool, 1)
            ones = [ST[b][MAXROW:MAXROW + 2, 8:10, :].bitcast(F32) for b in range(B)] + [
                pick[MAXROW:MAXROW + 2, :].bitcast(F32)]
            for i, m in enumerate(ones):
                pool.wait_ge(cleared_pool, 16 + i)
                nc.gpsimd.memset(m, 1.0).then_inc(cleared_pool, 1)
            pool.wait_ge(cleared_pool, 19)

        @block.scalar
        def _(act):
            for s in plan:
                kind, L, b = s[0], s[1], s[2] if len(s) > 2 else None
                if kind == "fold":
                    wait_tile(act, s)
                    nc.scalar.activation(w3vo[:, :], slot(s)[:, 0:C], ACT.Identity)
                    nc.scalar.activation(b3eff[:, :], slot(s)[:, HALF:HALF + 1], ACT.Identity,
                                         bias=w("b3o")).then_inc(read_act, 1)
                    act.wait_ge(sel_in, 16)
                    nc.scalar.activation(selr[:, :, :].rearrange("p t c -> p (t c)"), T[:, :],
                                         ACT.Identity).then_inc(consts_act, 1)
                elif kind in ("qk", "q", "k"):
                    wait_tile(act, s)
                    if kind == "qk":
                        act.wait_ge(signs_done, L + 1)
                        wait_stage_free(act, s)
                        nc.scalar.activation(Hs[:, :], slot(s), ACT.Identity, scale=w("lo_sign"),
                                             bias=lob[L][:, :]).then_inc(hi_done, 1)
                    elif L == 2 and kind == "q":
                        wait_stage_free(act, s)
                        nc.scalar.activation(Hs[:, :], slot(s), ACT.Identity).then_inc(hi_done, 1)
                    elif L == 2:
                        if b == 1:
                            act.wait_ge(stacks_in[0], stacks_count(2, 0) - 0)
                        nc.scalar.activation(HK[:, :], slot(s)[:, 0:NKV], ACT.Identity).then_inc(hi_done, 1)
                    else:
                        wait_ops_free(act, L, b)
                        k0 = 0 if kind == "q" else 8
                        nc.scalar.activation(ST[b][:, k0, :], slot(s), ACT.Identity,
                                             bias=w("b3" + kind)).then_inc(hi_done, 1)
                elif kind == "v" and L > 0:
                    wait_tile(act, s)
                    if L == 2:
                        act.wait_ge(cleared_pool, 19)
                        v = slot(s)[:, 0:2 * C].rearrange("p (r g h d) -> p r g h d", r=2, g=2, h=HG)
                        nc.scalar.activation(V2[b][:, :, 0, :, 0:D2], v[:, 0], ACT.Identity)
                        nc.scalar.activation(V2[b][:, :, 1, :, 0:D2], v[:, 1], ACT.Identity).then_inc(read_act, 1)
                    else:
                        if L == 3:
                            act.wait_ge(pv_done, pv_done_at[("B", 1, b, 0, 7)])
                        nc.scalar.activation(V13[b][:, :, :].rearrange("p t c -> p (t c)"), slot(s), ACT.Identity,
                                             scale=w("gam1") if L == 1 else 1.0).then_inc(read_act, 1)
                elif kind == "top":
                    wait_tile(act, s)
                    i = top_no[s] % 2
                    if top_no[s] >= 2:
                        p = list(top_no)[top_no[s] - 2]
                        act.wait_ge(maxrows_in[p[2]], max_count(*p[1:]))
                    rows = 64 if L == 2 else 16
                    nc.scalar.activation(ZR[0:rows, i, :], slot(s)[0:rows, 0:128], ACT.Identity).then_inc(read_act, 1)
                elif kind == "B":
                    n = b_no[s]
                    wait_tile(act, s)
                    if n >= NP:
                        p = b_order[n - NP]
                        act.wait_ge(pv_done, pv_done_at[p])
                        q = ("PV1", *p[1:4], max(p[4], 1))
                        if q in den_no:
                            act.wait_ge(den_acc, den_no[q])
                    nc.scalar.activation(P[:, n % NP, :], slot(s), ACT.Exp, scale=SCALE[L]).then_inc(read_act, 1)
                elif kind == "out":
                    u = s[1:]
                    act.wait_ge(pv_done, pv_done_at[("B", *u, 7)])
                    last = o_last.get(o_before[u])
                    if last and last[0] == "y":
                        wait_tile(act, last)
                    elif last:
                        wait_read(act, last)
                    nc.scalar.activation(O[o_tile[u]][:, :], acc[:, :], ACT.Identity).then_inc(acc_out, 1)
                elif kind == "dsum":
                    wait_tile(act, s)
                    wait_sum_free(act, s)
                    nc.scalar.activation(DS[:, :], slot(s), ACT.Identity).then_inc(read_act, 1)
                elif kind == "y" and L == 0:
                    wait_tile(act, s)
                    if x_upd_before(s):
                        act.wait_ge(x_upd, x_upd_before(s))
                    nc.scalar.activation(T[:, :], slot(s), ACT.Identity).then_inc(read_act, 1)
                elif kind == "rows":
                    wait_tile(act, s)
                    p = previous("bcast", s)
                    if p:
                        wait_tile(act, p)
                    nc.scalar.activation(RT[:, :], slot(s)[:, 0:128], ACT.Identity).then_inc(read_act, 1)
                elif kind == "norm":
                    act.wait_ge(coef_done, norm_no[s] + 1)
                    wait_norm_free(act, s)
                    nc.scalar.activation(XN[:, :], X[b][:, :], ACT.Identity, scale=ab[:, 0, 0:1],
                                         bias=ab[:, 0, 1:2]).then_inc(xn_done, 1)

        @block.vector
        def _(dve):
            links = [0]

            def link(ins):
                links[0] += 1
                ins.then_inc(dve_chain, 1)
                dve.wait_ge(dve_chain, links[0])

            nc.vector.memset(ST[0][:, 0:4, :].bitcast(F32), 0.0).then_inc(cleared_dve, 1)
            nc.vector.memset(eps[:, 0:1], EPS)
            link(nc.vector.memset(eps[:, 1:2], 16 * EPS))
            dve.wait_ge(w1_in, 16)
            nc.vector.tensor_tensor(lob[0][:, :], w("b0qk"), w("lo_sign"), ALU.mult).then_inc(signs_done, 1)
            link(nc.vector.tensor_tensor(w("w0o").rearrange("p (h e) -> p h e", h=H0),
                                         w("w0o").rearrange("p (h e) -> p h e", h=H0),
                                         w("gam0").unsqueeze(2).broadcast_to([128, H0, 32]), ALU.mult))
            nc.vector.tensor_tensor(gb0[:, :], w("gam0c"), w("b0o"), ALU.mult).then_inc(consts_ready, 1)
            for s in plan:
                kind, L, b = s[0], s[1], s[2] if len(s) > 2 else None
                if kind == "fold":
                    dve.wait_ge(w2_in, 16)
                    nc.vector.tensor_tensor(lob[1][:, :], w("b1qk"), w("lo_sign"), ALU.mult).then_inc(signs_done, 1)
                    nc.vector.tensor_tensor(gb1[:, :], w("gam1"), w("b1v"), ALU.mult).then_inc(consts_ready, 1)
                if kind in ("qk", "q", "k"):
                    dve.wait_ge(hi_done, hi_no[s] + 1)
                    wait_tile(dve, s)
                    if kind == "qk":
                        wait_stage_free(dve, s)
                        nc.vector.scalar_tensor_tensor(
                            out=Ls[:, :], in0=slot(s), scalar=w(f"b{L}qk"),
                            in1=Hs[:, :].bitcast(F32), op0=ALU.add, op1=ALU.add).then_inc(read_dve, 1)
                    elif L == 2 and kind == "q":
                        wait_stage_free(dve, s)
                        nc.vector.tensor_tensor(Ls[:, :], slot(s), Hs[:, :].bitcast(F32), ALU.subtract).then_inc(read_dve, 1)
                    elif L == 2:
                        if b == 1:
                            dve.wait_ge(stacks_in[0], stacks_count(2, 0))
                        nc.vector.tensor_tensor(LK[:, :], slot(s)[:, 0:NKV], HK[:, :].bitcast(F32),
                                                ALU.subtract).then_inc(read_dve, 1)
                    else:
                        k0 = 0 if kind == "q" else 8
                        wait_ops_free(dve, L, b)
                        nc.vector.scalar_tensor_tensor(
                            out=ST[b][:, k0 + 1, :], in0=slot(s), scalar=w("b3" + kind),
                            in1=ST[b][:, k0, :].bitcast(F32), op0=ALU.add, op1=ALU.subtract).then_inc(read_dve, 1)
                elif kind == "v" and L == 0:
                    wait_tile(dve, s)
                    dve.wait_ge(cleared_pool, 8)
                    nc.vector.tensor_tensor(
                        V0[b][:, :, :, 0:D0],
                        slot(s)[:, 0:NT * 16].rearrange("p (t h d) -> p h t d", t=NT, h=H0),
                        w("b0v").rearrange("p (h d) -> p h d", h=H0).unsqueeze(2).broadcast_to([128, H0, NT, D0]),
                        ALU.add).then_inc(read_dve, 1)
                elif kind == "A":
                    g, t = s[3], s[4]
                    u = split_no[("split", *s[1:4])]
                    wait_tile(dve, s)
                    if t == 0 and u >= 2:
                        dve.wait_ge(split_done, u - 1)
                    if L == 2:
                        nc.vector.tensor_reduce(out=NM[:, u % 2, 4 * t:4 * t + 4],
                                                in_=slot(s).rearrange("p (k r) -> p k r", k=4),
                                                op=ALU.max, axis=AX.X, negate=True).then_inc(read_dve, 1)
                    else:
                        nc.vector.tensor_reduce(out=NM[:, u % 2, t:t + 1], in_=slot(s), op=ALU.max, axis=AX.X,
                                                negate=True).then_inc(read_dve, 1)
                elif kind == "split":
                    u = split_no[s]
                    nk = 32 if L == 2 else 8
                    wait_read(dve, ("A", *s[1:4], 7))
                    if u >= 2:
                        wait_tile(dve, ("top", *list(split_no)[u - 2][1:]))
                    Z = ZT[:, u % 2, :, :].rearrange("p a k -> p (a k)")
                    link(nc.vector.tensor_copy(Z[:, 0:nk].bitcast(F32R), NM[:, u % 2, 0:nk]))
                    nc.vector.tensor_tensor(Z[:, nk:2 * nk], NM[:, u % 2, 0:nk], Z[:, 0:nk],
                                            ALU.subtract).then_inc(split_done, 1)
                elif kind == "den":
                    wait_tile(dve, s)
                    dve.wait_ge(cleared_pool, 14)
                    p = previous("rows", s)
                    if p:
                        wait_tile(dve, p)
                    nc.vector.reciprocal(RR[:, :], slot(s)[:, 0:32]).then_inc(read_dve, 1)
                    wait_read(dve, s)
                    link(nc.vector.tensor_copy(RC[:, 0:32].bitcast(F32R), RR[:, :]))
                    nc.vector.tensor_tensor(RC[:, 32:64], RR[:, :], RC[:, 0:32], ALU.subtract).then_inc(recip_done, 1)
                elif kind == "bcast":
                    g = s[3]
                    o = O[o_tile[(L, b, g)]]
                    wait_tile(dve, s)
                    if L == 0:
                        wait_read(dve, ("y", 0, b))
                        nc.vector.tensor_tensor(T[:, :], T[:, :], slot(s), ALU.mult).then_inc(read_dve, 1)
                        wait_read(dve, s)
                        dve.wait_ge(consts_ready, 1)
                        nc.vector.scalar_tensor_tensor(out=X[b][:, :], in0=T[:, :], scalar=gb0[:, 0:1], in1=X[b][:, :],
                                                       op0=ALU.add, op1=ALU.add).then_inc(x_upd, 1)
                    elif L == 2:
                        dve.wait_ge(acc_out, out_no[("out", L, b, g)] + 1)
                        nc.vector.tensor_tensor(o[:, :], o[:, :], slot(s), ALU.mult).then_inc(read_dve, 1)
                    else:
                        dve.wait_ge(acc_out, out_no[("out", L, b, g)] + 1)
                        if x_upd_before(s):
                            dve.wait_ge(x_upd, x_upd_before(s))
                        nc.vector.tensor_tensor(T[:, :], o[:, :], slot(s), ALU.mult).then_inc(read_dve, 1)
                        wait_read(dve, s)
                        if L == 1:
                            dve.wait_ge(consts_ready, 2)
                        else:
                            wait_read(dve, ("fold", 3))
                        nc.vector.scalar_tensor_tensor(out=X[b][:, :], in0=T[:, :],
                                                       scalar=gb1[:, 0:1] if L == 1 else b3eff[:, 0:1], in1=X[b][:, :],
                                                       op0=ALU.add, op1=ALU.add).then_inc(x_upd, 1)
                elif kind == "y" and L == 2:
                    wait_tile(dve, s)
                    nc.vector.tensor_tensor(X[b][:, :], slot(s), X[b][:, :], ALU.add).then_inc(read_dve, 1)
                elif s in den_no:
                    t = s[4]
                    n = b_no[("B", *s[1:])]
                    wait_read(dve, ("B", *s[1:]))
                    if t == 1:
                        wait_sum_free(dve, s)
                        first_in = P[:, (n - 1) % NP, :]
                    else:
                        dve.wait_ge(den_acc, den_no[s] - 1)
                        first_in = DS[:, :]
                    nc.vector.tensor_tensor(DS[:, :], first_in, P[:, n % NP, :], ALU.add).then_inc(den_acc, 1)
                elif kind == "stats":
                    ni = 2 if L == 2 else 1
                    wait_x(dve, L, b)
                    if L == 2:
                        wait_norm_free(dve, s)
                        xv = X[b][:, :].rearrange("c (m two) -> c m two", two=2)
                        nc.vector.tensor_tensor(KP, xv[:, :, 0], xv[:, :, 1], ALU.add)
                    nc.vector.bn_stats(bn[:, 0, :], X[b][:, 0:HALF])
                    link(nc.vector.bn_stats(bn[:, 1, :], X[b][:, HALF:N]))
                    if L == 2:
                        kv2 = KP.rearrange("c (i two j) -> c i two j", two=2, j=16)
                        nc.vector.tensor_tensor(KV[:, :].rearrange("c (i j) -> c i j", j=16),
                                                kv2[:, :, 0, :], kv2[:, :, 1, :], ALU.add)
                    link(nc.vector.bn_aggr(mv[:, 0, :], bn[:, 0:2, :]))
                    if L == 2:
                        link(nc.vector.bn_stats(bn[:, 2, :], KV[:, :]))
                        link(nc.vector.bn_aggr(mv[:, 1, :], bn[:, 2:3, :]))
                    link(nc.vector.tensor_tensor(nt[:, 0, 0:ni], mv[:, 0:ni, 0], mv[:, 0:ni, 0], ALU.mult))
                    nc.vector.tensor_tensor(mv[:, 0:ni, 1], mv[:, 0:ni, 1], nt[:, 0, 0:ni], ALU.add).then_inc(stats_done, 1)
                elif kind == "norm":
                    ni = 2 if L == 2 else 1
                    wait_tile(dve, s)
                    nc.vector.tensor_copy(gs[:, 0:ni, :], slot(s)[:, 0:2 * ni].rearrange("p (i k) -> p i k", k=2)).then_inc(read_dve, 1)
                    wait_read(dve, s)
                    mean, ex2 = gs[:, 0:ni, 0], gs[:, 0:ni, 1]
                    v, y, a, h = (nt[:, i, 0:ni] for i in range(1, 5))
                    link(nc.vector.tensor_tensor(a, mean, mean, ALU.mult))
                    link(nc.vector.tensor_tensor(v, ex2, a, ALU.subtract))
                    link(nc.vector.scalar_tensor_tensor(out=v, in0=v, scalar=0.0, in1=eps[:, 0:ni],
                                                        op0=ALU.max, op1=ALU.add))
                    nc.vector.tensor_scalar(h, v, -0.5, None, ALU.mult)
                    link(nc.vector.tensor_scalar(a.bitcast(I32), v.bitcast(I32), 1, None, ALU.arith_shift_right))
                    link(nc.vector.tensor_scalar(y.bitcast(I32), a.bitcast(I32), -1.0, float(RSQRT_SEED), ALU.mult, ALU.add))
                    for _ in range(3):
                        link(nc.vector.tensor_tensor(a, y, y, ALU.mult))
                        link(nc.vector.tensor_tensor(a, a, h, ALU.mult))
                        link(nc.vector.scalar_tensor_tensor(out=y, in0=a, scalar=1.5, in1=y, op0=ALU.add, op1=ALU.mult))
                    gn = w(f"gn{L}").rearrange("p (i k) -> p i k", k=2)
                    if norm_no[s]:
                        dve.wait_ge(xn_done, norm_no[s])
                    link(nc.vector.tensor_tensor(ab[:, 0:ni, 0], y, gn[:, 0:ni, 0], ALU.mult))
                    link(nc.vector.tensor_tensor(a, mean, ab[:, 0:ni, 0], ALU.mult))
                    nc.vector.tensor_tensor(ab[:, 0:ni, 1], gn[:, 0:ni, 1], a, ALU.subtract).then_inc(coef_done, 1)
                    if L == 2:
                        dve.wait_ge(coef_done, norm_no[s] + 1)
                        if b == 1:
                            wait_tile(dve, ("v", 2, 0))
                        nc.vector.tensor_scalar(KVN[:, :], KV[:, :], ab[:, 1, 0:1], ab[:, 1, 1:2],
                                                ALU.mult, ALU.add).then_inc(kvn_done, 1)

        @block.tensor
        def _(pe):
            halves = (slice(0, HALF), slice(HALF, N))

            def full(s, mm):
                mm.then_inc(tile_full, 1)

            for s in plan:
                kind, L, b = s[0], s[1], s[2] if len(s) > 2 else None
                if s in job and job[s] >= RING:
                    wait_read(pe, jobs[job[s] - RING])
                if kind == "fold":
                    pe.wait_ge(w2_in, 16)
                    nc.tensor.matmul(slot(s)[:, 0:C], w("w3v"), w("w3o"), start=True, stop=True)
                    full(s, nc.tensor.matmul(slot(s)[:, HALF:HALF + 1], w("w3o"), w("b3v"), start=True, stop=True))
                elif kind in ("qk", "q"):
                    if L in (0, 1):
                        if L == 0:
                            pe.wait_ge(w1_in, 16)
                        wait_x(pe, L, b)
                        for h in halves:
                            mm = nc.tensor.matmul(slot(s)[:, h], w(f"w{L}qk"), X[b][:, h], start=True, stop=True)
                    else:
                        pe.wait_ge(xn_done, norm_no[("norm", L, b)] + 1)
                        for h in halves:
                            mm = nc.tensor.matmul(slot(s)[:, h], w(f"w{L}q"), XN[:, h], start=True, stop=True)
                    full(s, mm)
                elif kind == "k":
                    if L == 2:
                        pe.wait_ge(kvn_done, b + 1)
                        full(s, nc.tensor.matmul(slot(s)[:, 0:NKV], w("w2k"), KVN[:, :], start=True, stop=True))
                    else:
                        for h in halves:
                            mm = nc.tensor.matmul(slot(s)[:, h], w("w3k"), XN[:, h], start=True, stop=True)
                        full(s, mm)
                elif kind == "v":
                    src, wv, width, tiles = {0: (X[b], w("w0v"), 16, NT), 1: (X[b], w("w1v"), C, NT),
                                             2: (KVN, w("w2v"), C, 2), 3: (XN, w3vo[:, :], C, NT)}[L]
                    if L == 3:
                        wait_read(pe, ("fold", 3))
                    for t in range(tiles):
                        mm = nc.tensor.matmul(slot(s)[:, width * t:width * (t + 1)], src[:, 128 * t:128 * (t + 1)], wv,
                                              start=True, stop=True)
                    full(s, mm)
                elif kind == "A":
                    g, t = s[3], s[4]
                    if t == 0:
                        pe.wait_ge(stacks_in[b], stacks_count(L, b))
                        if L == 2:
                            pe.wait_ge(cleared_pool, 19)
                    if L == 3:
                        wait_read(pe, ("q", 3, b))
                        wait_read(pe, ("k", 3, b))
                        for h in halves:
                            mm = nc.tensor.matmul(slot(s)[:, h], ST[b][:, 0, 128 * t:128 * (t + 1)], ST[b][:, 8, h],
                                                  start=True, stop=True)
                    elif L == 2:
                        head = HG * g + t // 2
                        k = ST[b][0:KROWS, 8:10, :].rearrange("p s n -> p (s n)")[:, NKV * head:NKV * (head + 1)]
                        for i in range(4):
                            kt = 4 * (t % 2) + i
                            mm = nc.tensor.matmul(slot(s)[:, NKV * i:NKV * (i + 1)],
                                                  ST[b][0:KROWS, head, 128 * kt:128 * (kt + 1)], k,
                                                  start=True, stop=True)
                    else:
                        ks, rs = (g, 4 + g) if L == 0 else (0, 4)
                        for h in halves:
                            mm = nc.tensor.matmul(slot(s)[:, h], ST[b][0:KROWS, ks, 128 * t:128 * (t + 1)],
                                                  ST[b][0:KROWS, rs, h], start=True, stop=True)
                    full(s, mm)
                elif kind == "top":
                    u = split_no[("split", *s[1:])]
                    nk = 32 if L == 2 else 8
                    pe.wait_ge(split_done, u + 1)
                    full(s, nc.tensor.transpose(slot(s)[0:2 * nk, 0:128],
                                                ZT[:, u % 2, :, :].rearrange("p a k -> p (a k)")[:, 0:2 * nk], w("ident")))
                elif kind == "B":
                    g, t = s[3], s[4]
                    if t == 0:
                        pe.wait_ge(maxrows_in[b], max_count(L, b, g))
                    if L == 3:
                        if t == 0:
                            pe.wait_ge(cleared_pool, 19)
                        tile = slice(128 * t, 128 * (t + 1))
                        for h in halves:
                            nc.tensor.matmul(slot(s)[:, h], pick[:, :], ST[b][0:KROWS, 2, h], start=True, stop=False)
                        for i, (r, k) in enumerate(((8, 0), (8, 1), (9, 0), (9, 1))):
                            for h in halves:
                                mm = nc.tensor.matmul(slot(s)[:, h], ST[b][:, r, tile], ST[b][:, k, h],
                                                      start=False, stop=i == 3)
                    else:
                        if L == 2:
                            head, rt = HG * g + t % 4, t // 4
                            ks = head
                            red = ST[b][0:KROWS, 8:10, :].rearrange("p s n -> p (s n)")[
                                :, NKV * head + 128 * rt:NKV * head + 128 * (rt + 1)]
                        else:
                            ks = g if L == 0 else 0
                            red = ST[b][0:KROWS, 4 + ks, 128 * t:128 * (t + 1)]
                        for h in halves:
                            mm = nc.tensor.matmul(slot(s)[:, h], red, ST[b][0:KROWS, ks, h], start=True, stop=True)
                    full(s, mm)
                elif kind in ("PV4", "PV1"):
                    g, t0 = s[3], s[4]
                    if t0 == 0:
                        if out_no[("out", L, b, g)]:
                            pe.wait_ge(acc_out, out_no[("out", L, b, g)])
                        if L == 0:
                            wait_read(pe, ("v", 0, b))
                        else:
                            wait_read(pe, ("v", L, b))
                    if kind == "PV4":
                        tiles = [("B", L, b, g, 4 * t0 + j) for j in range(4)]
                        wait_read(pe, tiles[3])
                        for h in halves:
                            for j, q in enumerate(tiles):
                                lhs = V0[b][:, g, 4 * t0 + j, :] if L == 0 else V2[b][:, g, t0, j, :]
                                mm = nc.tensor.matmul(acc[32 * j:32 * j + 32, h], lhs, P[:, b_no[q] % NP, h],
                                                      start=t0 == 0, stop=t0 == 1)
                                if h.start:
                                    mm.then_inc(pv_done, 1)
                    else:
                        q = ("B", L, b, g, t0)
                        wait_read(pe, q)
                        for h in halves:
                            mm = nc.tensor.matmul(acc[:, h], V13[b][:, t0, :], P[:, b_no[q] % NP, h],
                                                  start=t0 == 0, stop=t0 == 7)
                        mm.then_inc(pv_done, 1)
                elif kind == "den":
                    g = s[3]
                    if L == 0:
                        wait_read(pe, ("dsum", 0, b))
                    elif L == 2:
                        pe.wait_ge(acc_out, out_no[("out", L, b, g)] + 1)
                    else:
                        pe.wait_ge(den_acc, den_no[("PV1", L, b, g, 7)])
                    for t in range(NT):
                        src, sel = {0: (DS, w("pick4")), 1: (DS, w("ones4")), 2: (O[o_tile[(L, b, g)]], w("sel2")),
                                    3: (DS, w("ones4"))}[L]
                        mm = nc.tensor.matmul(slot(s)[:, 4 * t:4 * t + 4], src[:, 128 * t:128 * (t + 1)], sel,
                                              start=True, stop=True)
                    full(s, mm)
                elif kind == "rows":
                    pe.wait_ge(recip_done, recip_no[("den", *s[1:])] + 1)
                    full(s, nc.tensor.transpose(slot(s)[:, 0:128], RC[:, :], w("ident")))
                elif kind == "bcast":
                    wait_read(pe, ("rows", *s[1:]))
                    pe.wait_ge(consts_act, 1)
                    for t in range(NT):
                        mm = nc.tensor.matmul(slot(s)[:, 128 * t:128 * (t + 1)], selr[:, t, :], RT[:, :],
                                              start=True, stop=True)
                    full(s, mm)
                elif kind == "dsum":
                    pe.wait_ge(w2_in, 16)
                    pe.wait_ge(acc_out, out_no[("out", 0, b, 3)] + 1)
                    for h in halves:
                        for i in range(H0):
                            mm = nc.tensor.matmul(slot(s)[32 * i:32 * i + 32, h], w("den0"), O[o_tile[(0, b, i)]][:, h],
                                                  start=True, stop=True)
                    full(s, mm)
                elif kind == "y" and L == 0:
                    pe.wait_ge(consts_ready, 1)
                    pe.wait_ge(acc_out, out_no[("out", 0, b, 3)] + 1)
                    for h in halves:
                        for i in range(H0):
                            mm = nc.tensor.matmul(slot(s)[32 * i:32 * i + 32, h], w("w0o")[:, 32 * i:32 * i + 32],
                                                  O[o_tile[(0, b, i)]][:, h], start=True, stop=True)
                    full(s, mm)
                elif kind == "y":
                    wait_read(pe, ("bcast", 2, b, 1))
                    for h in halves:
                        for g in range(2):
                            mm = nc.tensor.matmul(slot(s)[:, h], w("w2p")[:, 128 * g:128 * (g + 1)],
                                                  O[o_tile[(2, b, g)]][:, h], start=g == 0, stop=g == 1)
                    full(s, mm)
                elif kind == "norm":
                    pe.wait_ge(stats_done, norm_no[s] + 1)
                    ni = 2 if L == 2 else 1
                    full(s, nc.tensor.matmul(slot(s)[:, 0:2 * ni], w("avg16" if L == 2 else "avg4"),
                                             mv[:, 0:ni, :].rearrange("p i k -> p (i k)"), start=True, stop=True))


def pack(layout, parts):
    import numpy as np

    at, n = columns(layout)
    out = np.zeros((128, n), np.float32)
    for name, a in parts.items():
        out[:a.shape[0], at[name][0]:at[name][0] + a.shape[1]] = a
    return out


def kernel(**inputs):
    import numpy as np
    import concourse.bacc as bacc
    from concourse.bass_utils import run_bass_kernel_spmd

    a = {k: np.asarray(v) for k, v in inputs.items()}

    def col(v):
        return v.reshape(-1, 1)

    def dh(wt, h, d):
        return wt.reshape(h, d, C).transpose(1, 0, 2).reshape(h * d, C)

    def dhb(bias, h, d):
        return bias.reshape(h, d).transpose(1, 0).reshape(-1)

    w0qk = np.concatenate([dh(a["L0_conv_Wk"], H0, D0)] * 4 + [dh(a["L0_conv_Wq"], H0, D0)] * 4).T
    b0qk = col(np.concatenate([dhb(a["L0_conv_bk"], H0, D0)] * 4 + [dhb(a["L0_conv_bq"], H0, D0)] * 4))
    lo_sign = np.zeros((2, 4, 16, 1), np.float32)
    lo_sign[0, 1] = lo_sign[0, 3] = lo_sign[1, 2] = lo_sign[1, 3] = -1
    w0o = np.zeros((4, 32, H0, 32), np.float32)
    for j in range(4):
        w0o[j, 0:D0] = a["L0_conv_Wo"].transpose(2, 0, 1)
    den0 = np.zeros((4, 32, 32), np.float32)
    den0[:, D0] = 1
    pick4 = np.zeros((4, 32, 4), np.float32)
    for h in range(4):
        pick4[h, 0, h] = 1
    gam0 = a["L0_conv_gamma"]
    first = pack(FIRST, {
        "w0qk": w0qk, "b0qk": b0qk,
        "w0v": a["L0_conv_Wv"].reshape(16, C).T,
        "b0v": np.broadcast_to(a["L0_conv_bv"].reshape(1, 16), (128, 16)),
        "lo_sign": lo_sign.reshape(128, 1),
        "gam0": np.broadcast_to(gam0.reshape(1, 4), (128, 4)),
        "gam0c": col(np.repeat(gam0, 32)), "b0o": col(a["L0_conv_bo"]),
        "w0o": w0o.reshape(128, 128), "ident": np.eye(128, dtype=np.float32)})
    sel = np.zeros((NT, 4, NT, 4, 32), np.float32)
    for t in range(NT):
        for h in range(4):
            sel[t, h, t, h] = 1
    selp = np.zeros((128, 1024), np.float32)
    selp[0:32] = selp[32:64] = sel.reshape(32, 1024)
    w2p = np.zeros((HG, 32, 2, C), np.float32)
    w2p[:, 0:D2] = a["L2_conv_wproj"].T.reshape(2, HG, D2, C).transpose(1, 2, 0, 3)
    sel2 = np.zeros((HG, 32, HG), np.float32)
    for h in range(HG):
        sel2[h, D2, h] = 1
    qkv, qkvb = a["L3_conv_qkv_w"], a["L3_conv_qkv_b"]

    def blocks(n):
        m = np.zeros((C // n, n, C // n, n), np.float32)
        for i in range(C // n):
            m[i, :, i, :] = 1.0 / n
        return m.reshape(C, C)

    rest = pack(REST, {
        "den0": den0.reshape(128, 32), "pick4": pick4.reshape(128, 4),
        "w1qk": np.concatenate([a["L1_conv_wq"]] * 4 + [a["L1_conv_wk"]] * 4).T,
        "b1qk": col(np.concatenate([a["L1_conv_bq"]] * 4 + [a["L1_conv_bk"]] * 4)),
        "w1v": a["L1_conv_wv"].T, "b1v": col(a["L1_conv_bv"]),
        "gam1": np.broadcast_to(a["L1_conv_gamma"].reshape(1, 1), (128, 1)),
        "w2q": dh(a["L2_conv_wq"], H2, D2).T, "w2k": dh(a["L2_conv_wk"], H2, D2).T, "w2v": a["L2_conv_wv"].T,
        "w2p": w2p.reshape(128, 256),
        "gn2": np.stack([a["L2_conv_gnq_w"], a["L2_conv_gnq_b"], a["L2_conv_gnk_w"], a["L2_conv_gnk_b"]], 1),
        "avg16": blocks(16), "sel2": sel2.reshape(128, 4), "ones4": np.ones((128, 4), np.float32),
        "w3q": qkv[0:C].T, "w3k": qkv[C:2 * C].T, "w3v": qkv[2 * C:], "w3o": a["L3_conv_out_w"].T,
        "b3q": col(qkvb[0:C]), "b3k": col(qkvb[C:2 * C]), "b3v": col(qkvb[2 * C:]), "b3o": col(a["L3_conv_out_b"]),
        "gn3": np.stack([a["L3_conv_gn_w"], a["L3_conv_gn_b"]], 1), "avg4": blocks(4)})
    x = np.ascontiguousarray(a["x"]).reshape(B, C, N)

    nc = bacc.Bacc("TRN2", target_bir_lowering=False, num_devices=1)
    arrays = {"x": x, "w_first": first, "w_rest": rest, "row_selector": selp}
    args = [nc.dram_tensor(n, v.shape, F32, kind="ExternalInput").ap() for n, v in arrays.items()]
    out = nc.dram_tensor("y", (B, C, N), F32, kind="ExternalOutput").ap()
    attention_layers(nc, *args, out)
    r = run_bass_kernel_spmd(nc, [arrays], core_ids=[0])
    return r.results[0]["y"].reshape(B, C, 32, 32)
```

```python
from contextlib import ExitStack

import concourse.bass as bass
from concourse import mybir

F32 = mybir.dt.float32
F32R = mybir.dt.float32r
I32 = mybir.dt.int32
ALU = mybir.AluOpType
ACT = mybir.ActivationFunctionType
AX = mybir.AxisListType

B, C, N = 2, 128, 1024
NT = N // 128
HALF = 512
NKV = 256
H0, D0 = 4, 4
D1 = 16
H2, D2 = 8, 16
HG = 4
MAXROW = 64
KROWS = 128
RING = 3
NP = 8
POOL_SUM = 6
O_TILES = 5
EPS = 1e-5
SCALE = {0: 1.0, 1: 1.0, 2: float(D2) ** -0.5, 3: float(C) ** -0.5}
RSQRT_SEED = 0x5F3759DF

FIRST = [("w0qk", 128), ("b0qk", 1), ("lo_sign", 1), ("w0v", 16), ("b0v", 16)]
REST = [("gam0", 4), ("gam0c", 1), ("b0o", 1), ("w0o", 128), ("ident", 128), ("den0", 32), ("pick4", 92), ("w1qk", 128), ("b1qk", 1), ("w1v", 128),
        ("b1v", 1), ("gam1", 1),
        ("w2q", 128), ("w2k", 128), ("w2v", 128), ("w2p", 256), ("gn2", 4), ("avg16", 128),
        ("sel2", 92), ("ones4", 92), ("lo_rows", 1), ("w3q", 128), ("w3k", 128), ("w3v", 128), ("w3o", 128), ("b3q", 1),
        ("b3k", 1), ("b3v", 1), ("b3o", 1), ("gn3", 2), ("avg4", 128)]


def columns(layout):
    at, out = 0, {}
    for name, width in layout:
        out[name] = (at, width)
        at += width
    return out, at


UNITS = [(0, 0, 0), (0, 0, 1), (0, 0, 2), (0, 0, 3), (0, 1, 0), (0, 1, 1), (1, 0, 0), (0, 1, 2), (0, 1, 3),
         (2, 0, 0), (2, 0, 1), (1, 1, 0), (3, 0, 0), (2, 1, 0), (2, 1, 1), (3, 0, 1), (3, 1, 0)]
TILES = {(L, b, g): range(8) for L, b, g in UNITS}
TILES[(3, 0, 0)], TILES[(3, 0, 1)] = range(0, 4), range(4, 8)


def groups(L, b):
    return len([u for u in TILES if u[:2] == (L, b)])


ORDER = (
    "NAAAAAAANAVAATAAA"
    "BABABAABAVBAPTAABPAABBA"
    "BAABPABABPTABAPABAPBABP"
    "BABAABAPTBPPABBPABBP"
    "BBAPBBAPAPABPBABBAPTAAVPPP"
    "BAEEAEBABEBABPNVABABBPATAAAPPPA"
    "BABABABABBAPTBABAPAPA"
    "BPPBABPAPPBAPPAPBAABPPAPBAPATPBPPAPA"
    "BPAAPEPBBBAEBBTNPBBNPP"
    "BPNBPBNBBBBPBVPPAAPAAPAEAAAAEATEA"
    "BEBBBAAANAVABABBAPTABAAP"
    "BABABAPBAPPABBPBBAETPPPPE"
    "BEBYEPBEPPPNBNPPBPNNBPPAAPABPAPPBAPPAAEPAPEAVNTN"
    "BNPNBBPBAAPAVAAPAAPAPAPATAAPPA"
    "BABABABABAPTBBBP"
    "BBBPBPPBBBPPBEPPPEEYEEN"
    "BNBBNNBAAPAAPPAPAAAAPVPTPP"
    "BBBPBEPBPBEPPPPPBPPBPPPPPPEPPE"
)


def prologue(L, b):
    if L in (0, 1):
        return [("qk", L, b), ("v", L, b)]
    return [("stats", L, b), ("norm", L, b), ("q", L, b), ("k", L, b), ("v", L, b)]


def epilogue(L, b, g):
    if L != 2 and g < groups(L, b) - 1:
        return []
    if L == 0:
        return [("dsum", L, b), ("y", L, b), ("den", L, b, g), ("bcast", L, b, g)]
    if L == 2 and g == 1:
        return [("den", L, b, g), ("bcast", L, b, g), ("y", L, b)]
    return [("den", L, b, g), ("bcast", L, b, g)]


def last_step(L, b):
    return ("y", L, b) if L == 2 else ("bcast", L, b, groups(L, b) - 1)


def build_plan():
    steps = {c: [] for c in "ATBPENVY"}
    for L, b, g in UNITS:
        if g == 0:
            for s in prologue(L, b):
                steps["V" if s[0] == "v" else "N"].append(s)
        if L in (0, 2) or g == 0:
            steps["A"] += [("A", L, b, g, t) for t in range(8)] + [("split", L, b, g)]
            steps["T"] += [("top", L, b, g)]
        steps["B"] += [("B", L, b, g, t) for t in TILES[(L, b, g)]]
        steps["P"] += [("PV4", L, b, g, i, h) for i in range(2) for h in range(2)] if L in (0, 2) else [
            ("PV1", L, b, g, t, h) for t in TILES[(L, b, g)] for h in range(2)]
        steps["P"] += [("out", L, b, g)]
        steps["E"] += epilogue(L, b, g)
        if L == 2 and g == 1:
            steps["Y"].append(("ya", L, b))
    steps["V"].insert(2, ("fold", 3))
    following = {c: iter(s) for c, s in steps.items()}
    return [next(following[c]) for c in ORDER]


def attention_layers(nc, x, first, rest, sel, out):
    plan = build_plan()
    assert len(set(plan)) == len(plan)

    def last_reader(s):
        kind, L = s[0], s[1]
        if kind in ("A", "norm", "den", "bcast", "qk", "q", "k") or (kind, L) in (("v", 0), ("y", 2)):
            return "dve"
        if kind in ("B", "top", "fold", "dsum") or (kind, L) in (("v", 1), ("v", 2), ("v", 3), ("y", 0)):
            return "act"
        return None

    complete = {s: n + 1 for n, s in enumerate([s for s in plan if last_reader(s)])}
    jobs = [("y", 2, s[2]) if s[0] == "ya" else s for s in plan if (s in complete and s[:2] != ("y", 2)) or s[0] == "ya"]
    job = {s: n for n, s in enumerate(jobs)}
    read = {}
    for who in ("dve", "act"):
        for n, s in enumerate([s for s in complete if last_reader(s) == who]):
            read[s] = n + 1

    def number(kinds, layers=(0, 1, 2, 3)):
        return {s: n for n, s in enumerate([s for s in plan if s[0] in kinds and s[1] in layers])}

    b_no = number(("B",))
    b_order = list(b_no)
    hi_no = number(("qk", "q", "k"))
    half_no = {s: n for n, s in enumerate([s for s in hi_no if s[:2] != ("k", 2)])}
    stage = [s for s in plan if s[0] in ("qk", "q") and s[1] < 3]
    top_no = number(("top",))
    split_no = number(("split",))
    out_no = number(("out",))
    x_no = {}
    for s in plan:
        if s[0] == "bcast" and s[1] != 2 and s == last_step(s[1], s[2]):
            x_no[(s[1], s[2])] = len(x_no) + 1
    recip_no = number(("den",))
    den_ops = [s for s in plan if s[0] == "PV1" and s[4] > 0 and s[5] == 0]
    den_no = {s: n + 1 for n, s in enumerate(den_ops)}
    o_last = {(L, b, g): ("y", L, b) if L in (0, 2) else ("bcast", L, b, groups(L, b) - 1) for L, b, g in UNITS}
    o_tile, o_before, free, held = {}, {}, [(i, None) for i in range(O_TILES)], []
    for s in plan:
        if s[0] == "out" and s[1] in (1, 3) and s[3]:
            o_tile[s[1:]] = o_tile[(*s[1:3], 0)]
        elif s[0] == "out":
            tile, before = free.pop(0)
            o_tile[s[1:]], o_before[s[1:]] = tile, before
            held.append(s[1:])
        for u in [u for u in held if o_last[u] == s]:
            held.remove(u)
            free.append((o_tile[u], u))
    pv_done_at = {}
    n = 0
    for s in plan:
        if s[0] in ("PV4", "PV1") and s[5] == 1:
            n += 1
            for t in range(4 * s[4], 4 * s[4] + 4) if s[0] == "PV4" else [s[4]]:
                pv_done_at[("B", *s[1:4], t)] = n

    col1, n1 = columns(FIRST)
    col2, n2 = columns(REST)

    with ExitStack() as ctx:
        def sb(name, shape, dt=F32):
            return ctx.enter_context(nc.sbuf_tensor(name, shape, dt))

        def sem(name):
            return ctx.enter_context(nc.semaphore(name))

        w1 = sb("w1", [128, n1])
        w2 = sb("w2", [128, n2])
        selr = sb("head_rows_to_channels", [128, NT, C], F32R)

        def w(name):
            a, width = (col1 if name in col1 else col2)[name]
            return (w1 if name in col1 else w2)[:, a:a + width]

        X = [sb(f"x{b}", [C, N]) for b in range(B)]
        ST = [sb(f"score_ops{b}", [128, 10, N], F32R) for b in range(B)]
        Hs = sb("stage_hi", [128, N], F32R)
        Ls = sb("stage_lo", [128, N], F32R)
        HK = sb("stage_k_hi", [128, NKV], F32R)
        LK = sb("stage_k_lo", [128, NKV], F32R)
        P = sb("probs", [128, NP, N])
        V0 = [sb(f"v0_{b}", [128, H0, NT, 32]) for b in range(B)]
        V2 = [sb(f"v2_{b}", [128, 2, 2, HG, 32]) for b in range(B)]
        V13 = [sb(f"v13_{b}", [128, NT, C]) for b in range(B)]
        O = [sb(f"attn_out{i}", [128, N]) for i in range(O_TILES)]
        DS = sb("prob_sum", [128, N])
        T = sb("tmp", [128, N])
        XN = sb("x_norm", [C, N])
        KV = sb("kv_pool", [C, NKV])
        KP = XN[:, 0:512]
        KVN = sb("kv_norm", [C, NKV])
        unused = XN[:, HALF:N].bitcast(mybir.dt.bfloat16)
        NM = sb("neg_max", [128, 2, 32])
        ZT = sb("max_halves", [128, 2, 2, 32])
        ZR = sb("max_rows", [64, 2, 128])
        RR = sb("recips", [64, 128])
        RH = sb("recips_hi", [64, 128], F32R)
        RT = sb("recip_rows", [128, 128], F32R)
        lob = [sb(f"lo_bias{L}", [128, 1]) for L in (0, 1)]
        const = sb("const_rows", [4, N])
        pick = sb("max_picker", [KROWS, 128], F32R)
        w3vo = sb("w3vo", [C, C])
        b3eff = sb("b3eff", [C, 1])
        gb0 = sb("gamma_bo", [C, 1])
        gb1 = sb("gamma_bv", [C, 1])
        bn = sb("bn_parts", [C, 6])
        mv = sb("mean_var", [C, 2, 2])
        gs = sb("group_stats", [C, 2, 2])
        nt = sb("norm_tmp", [C, 6, 2])
        ab = sb("norm_scale_shift", [C, 2, 2])
        eps = sb("eps", [C, 2])

        ps = ctx.enter_context(nc.psum_tensor("products", [128, RING, N], F32))
        acc = ctx.enter_context(nc.psum_tensor("attn_acc", [128, N], F32))

        x_in = [sem(f"x_in{b}") for b in range(B)]
        w1_in, w2_in, sel_in = sem("w1_in"), sem("w2_in"), sem("sel_in")
        cleared_dve, cleared_pool = sem("cleared_dve"), sem("cleared_pool")
        consts_ready, consts_act = sem("consts_ready"), sem("consts_act")
        tile_full = sem("tile_full")
        read_dve, read_act = sem("tile_read_dve"), sem("tile_read_act")
        signs_done = sem("signs_done")
        half_full = sem("half_full")
        hi_half = sem("hi_half")
        hi_done = sem("hi_done")
        stacks_in = [sem(f"stacks_in{b}") for b in range(B)]
        stacks_late = [sem(f"stacks_late{b}") for b in range(B)]
        split_done = sem("split_done")
        maxrows_in = [sem(f"maxrows_in{b}") for b in range(B)]
        pv_done = sem("pv_done")
        den_acc = sem("den_acc")
        acc_out = sem("acc_out")
        recip_done = sem("recip_done")
        x_upd = sem("x_upd")
        stats_done, squares_done = sem("stats_done"), sem("squares_done")
        act_chain = sem("act_chain")
        coef_done = sem("coef_done")
        xn_half = sem("xn_half")
        xn_done, kvn_done = sem("xn_done"), sem("kvn_done")
        dve_chain = sem("dve_chain")
        out_done = sem("out_done")

        def slot(s):
            return ps[:, job[s] % RING, :]

        def wait_tile(eng, s):
            eng.wait_ge(tile_full, complete[s])

        def wait_read(eng, s):
            eng.wait_ge(read_dve if last_reader(s) == "dve" else read_act, read[s])

        def wait_x(eng, L, b):
            if L == 0:
                eng.wait_ge(x_in[b], 16)
            elif L == 3:
                wait_read(eng, ("y", 2, b))
            else:
                eng.wait_ge(x_upd, x_no[(L - 1, b)])

        stack_dmas = {0: 3, 1: 3, 2: 9}

        def stacks_count(L, b):
            return 16 * sum(stack_dmas[i] for i in range(min(L, 2) + 1))

        def wait_stage_free(eng, s):
            i = stage.index(s)
            if i:
                p = stage[i - 1]
                eng.wait_ge(stacks_in[p[2]], stacks_count(p[1], p[2]))
                if p[1] == 2:
                    eng.wait_ge(stacks_late[p[2]], 64)

        def wait_ops_free(eng, L, b):
            if L == 0:
                eng.wait_ge(cleared_pool, 3 + b)
                eng.wait_ge(cleared_dve, 1)
            else:
                wait_tile(eng, ("B", L - 1, b, groups(L - 1, b) - 1, 7))

        def max_count(L, b, g):
            order = [s for s in top_no if s[2] == b]
            return 16 * (order.index(("top", L, b, g)) + 1)

        def previous(kind, s):
            found = [p for p in plan[:plan.index(s)] if p[0] == kind]
            return found[-1] if found else None

        def wait_sum_free(eng, s):
            p = [p for p in plan[:plan.index(s)] if p[0] == "den" and p[1] != 2]
            if p:
                wait_tile(eng, p[-1])

        def wait_norm_free(eng, s):
            p = [p for p in plan[:plan.index(s)] if p[:2] in (("q", 2), ("v", 3))]
            if p:
                wait_tile(eng, p[-1])

        def x_upd_before(s):
            return len([p for p in plan[:plan.index(s)] if p[0] == "bcast" and p[1] != 2])

        norm_no = number(("norm",))
        halves = (slice(0, HALF), slice(HALF, N))

        def sum_exps(engine, eng, s):
            n = b_no[("B", *s[1:5])]
            wait_read(eng, ("B", *s[1:5]))
            if s[4] == 1:
                wait_sum_free(eng, s)
                first_in = P[:, (n - 1) % NP, :]
            else:
                eng.wait_ge(den_acc, den_no[s] - 1)
                first_in = DS[:, :]
            engine.tensor_tensor(DS[:, :], first_in, P[:, n % NP, :], ALU.add).then_inc(den_acc, 1)

        block = ctx.enter_context(nc.Block())

        @block.sync
        def _(sp):
            sp.dma_start(w1[:, :], first).then_inc(w1_in, 16)
            sp.dma_start(X[0][:, :], x[0]).then_inc(x_in[0], 16)
            sp.dma_start(X[1][:, :], x[1]).then_inc(x_in[1], 16)
            sp.dma_start(w2[:, :], rest).then_inc(w2_in, 16)
            sp.dma_start(T[:, :], sel).then_inc(sel_in, 16)

            def spread_q(b, g, done):
                for r, src in enumerate((Hs, Ls, Hs, Ls)):
                    sp.dma_start(ST[b][D2 * r:D2 * r + D2, HG * g:HG * g + HG, :].bitcast(F32),
                                 src[64 * g:64 * g + 64, :].bitcast(F32)).then_inc(done[b], 16)

            def spread_k(b):
                for r, src in enumerate((HK, HK, LK, LK)):
                    dst = ST[b][D2 * r:D2 * r + D2, 8:10, :].bitcast(F32).rearrange("p s n -> p (s n)")
                    sp.dma_start(dst.rearrange("p (h n) -> p h n", h=H2),
                                 src[:, :].bitcast(F32)).then_inc(stacks_in[b], 16)

            for s in plan:
                kind, L, b = s[0], s[1], s[2] if len(s) > 2 else None
                S = ST[b][:, :, :].bitcast(F32) if b is not None else None
                if kind == "qk" or (kind in ("q", "k") and L == 2):
                    wait_ops_free(sp, L, b)
                    mr = S[MAXROW:MAXROW + 2]
                    if kind == "qk" and L == 0:
                        sp.dma_start(mr[:, 4:8, :], const[2:4, :].unsqueeze(1).broadcast_to([2, 4, N])).then_inc(stacks_in[b], 16)
                    elif kind == "qk":
                        sp.dma_start(mr[:, 0, :], const[0:2, :]).then_inc(stacks_in[b], 16)
                    elif kind == "q":
                        sp.dma_start(mr[:, 0:H2, :], const[0:2, :].unsqueeze(1).broadcast_to([2, H2, N])).then_inc(stacks_in[b], 16)
                        sp.wait_ge(hi_done, hi_no[s] + 1)
                    wait_read(sp, s)
                if kind == "qk":
                    rows, heads = (4 * D0, H0) if L == 0 else (4 * D1, 1)
                    for s0, r0 in ((0, 0), (4, 64)):
                        sp.dma_start(S[0:rows, s0:s0 + heads, :], Ls[r0:r0 + 64, :].bitcast(F32)).then_inc(stacks_in[b], 16)
                elif kind == "q" and L == 2:
                    spread_q(b, 0, stacks_in)
                elif kind == "k" and L == 2:
                    spread_k(b)
                    spread_q(b, 1, stacks_late)
                elif kind == "top":
                    g = s[3]
                    i = top_no[s] % 2
                    wait_read(sp, s)
                    k0, kn = {0: (g, 1), 1: (0, 1), 2: (HG * g, HG), 3: (2, 1)}[L]
                    sp.dma_start(S[MAXROW:MAXROW + 2, k0:k0 + kn, :], ZR[0:16 * kn, i, :]).then_inc(maxrows_in[b], 16)
                elif kind == "bcast" and L == 3:
                    sp.wait_ge(x_upd, x_no[(3, b)])
                    sp.dma_start(out[b], X[b][:, :]).then_inc(out_done, 16)
            sp.wait_ge(out_done, 16 * B)

        @block.gpsimd
        def _(pool):
            nc.gpsimd.memset(const[:, :], 1.0).then_inc(cleared_pool, 1)
            pool.wait_ge(cleared_pool, 1)
            nc.gpsimd.memset(const[0:2, :], 0.0).then_inc(cleared_pool, 1)
            nc.gpsimd.memset(ST[0][:, 4:8, :].bitcast(F32), 0.0).then_inc(cleared_pool, 1)
            nc.gpsimd.memset(ST[1][:, 0:8, :].bitcast(F32), 0.0).then_inc(cleared_pool, 1)
            for b in range(B):
                nc.gpsimd.memset(V0[b][:, :, :, :], 0.0).then_inc(cleared_pool, 1)
            pool.wait_ge(cleared_pool, 6)
            for b in range(B):
                nc.gpsimd.memset(V0[b][:, :, :, D0:D0 + 1], 1.0).then_inc(cleared_pool, 1)
            for b in range(B):
                nc.gpsimd.memset(ST[b][:, 8:10, :].bitcast(F32), 0.0).then_inc(cleared_pool, 1)
                nc.gpsimd.memset(V2[b][:, :, :, :, :], 0.0).then_inc(cleared_pool, 1)
            nc.gpsimd.memset(pick[:, :].bitcast(F32), 0.0).then_inc(cleared_pool, 1)
            nc.gpsimd.memset(RT[:, :].bitcast(F32), 0.0).then_inc(cleared_pool, 1)
            pool.wait_ge(cleared_pool, 14)
            for b in range(B):
                nc.gpsimd.memset(V2[b][:, :, :, :, D2:D2 + 1], 1.0).then_inc(cleared_pool, 1)
            ones = [ST[b][MAXROW:MAXROW + 2, 8:10, :].bitcast(F32) for b in range(B)] + [
                pick[MAXROW:MAXROW + 2, :].bitcast(F32)]
            for i, m in enumerate(ones):
                pool.wait_ge(cleared_pool, 16 + i)
                nc.gpsimd.memset(m, 1.0).then_inc(cleared_pool, 1)
            pool.wait_ge(cleared_pool, 19)
            for s in plan:
                if s in den_no and s[4] < POOL_SUM:
                    sum_exps(nc.gpsimd, pool, s)

        @block.scalar
        def _(act):
            for s in plan:
                kind, L, b = s[0], s[1], s[2] if len(s) > 2 else None
                if kind == "fold":
                    wait_tile(act, s)
                    nc.scalar.activation(w3vo[:, :], slot(s)[:, 0:C], ACT.Identity)
                    nc.scalar.activation(b3eff[:, :], slot(s)[:, HALF:HALF + 1], ACT.Identity,
                                         bias=w("b3o")).then_inc(read_act, 1)
                    act.wait_ge(sel_in, 16)
                    nc.scalar.activation(selr[:, :, :].rearrange("p t c -> p (t c)"), T[:, :],
                                         ACT.Identity).then_inc(consts_act, 1)
                elif kind in ("qk", "q", "k"):
                    if s not in half_no:
                        wait_tile(act, s)
                        if b == 1:
                            act.wait_ge(stacks_in[0], stacks_count(2, 0))
                        nc.scalar.activation(HK[:, :], slot(s)[:, 0:NKV], ACT.Identity).then_inc(hi_done, 1)
                        continue
                    for h in halves:
                        if h.start == 0:
                            act.wait_ge(half_full, half_no[s] + 1)
                            if kind == "qk":
                                act.wait_ge(signs_done, L + 1)
                            if L == 3:
                                wait_ops_free(act, L, b)
                            else:
                                wait_stage_free(act, s)
                        else:
                            wait_tile(act, s)
                        if kind == "qk":
                            hi = nc.scalar.activation(Hs[:, h], slot(s)[:, h], ACT.Identity, scale=w("lo_sign"),
                                                      bias=lob[L][:, :])
                        elif L == 2:
                            hi = nc.scalar.activation(Hs[:, h], slot(s)[:, h], ACT.Identity)
                        else:
                            hi = nc.scalar.activation(ST[b][:, 0 if kind == "q" else 8, h], slot(s)[:, h],
                                                      ACT.Identity, bias=w("b3" + kind))
                        hi.then_inc(hi_done if h.start else hi_half, 1)
                elif kind == "v" and L > 0:
                    wait_tile(act, s)
                    if L == 2:
                        act.wait_ge(cleared_pool, 19)
                        v = slot(s)[:, 0:2 * C].rearrange("p (r g h d) -> p r g h d", r=2, g=2, h=HG)
                        nc.scalar.activation(V2[b][:, :, 0, :, 0:D2], v[:, 0], ACT.Identity)
                        nc.scalar.activation(V2[b][:, :, 1, :, 0:D2], v[:, 1], ACT.Identity).then_inc(read_act, 1)
                    else:
                        if L == 3:
                            act.wait_ge(pv_done, pv_done_at[("B", 1, b, groups(1, b) - 1, 7)])
                        nc.scalar.activation(V13[b][:, :, :].rearrange("p t c -> p (t c)"), slot(s), ACT.Identity,
                                             scale=w("gam1") if L == 1 else 1.0).then_inc(read_act, 1)
                elif kind == "top":
                    wait_tile(act, s)
                    i = top_no[s] % 2
                    if top_no[s] >= 2:
                        p = list(top_no)[top_no[s] - 2]
                        act.wait_ge(maxrows_in[p[2]], max_count(*p[1:]))
                    rows = 64 if L == 2 else 16
                    nc.scalar.activation(ZR[0:rows, i, :], slot(s)[0:rows, 0:128], ACT.Identity).then_inc(read_act, 1)
                elif kind == "B":
                    n = b_no[s]
                    wait_tile(act, s)
                    if n >= NP:
                        p = b_order[n - NP]
                        act.wait_ge(pv_done, pv_done_at[p])
                        q = ("PV1", *p[1:4], max(p[4], 1), 0)
                        if q in den_no:
                            act.wait_ge(den_acc, den_no[q])
                    nc.scalar.activation(P[:, n % NP, :], slot(s), ACT.Exp, scale=SCALE[L]).then_inc(read_act, 1)
                elif kind == "out" and (L in (0, 2) or s[3] == 0):
                    u = s[1:]
                    act.wait_ge(pv_done, pv_done_at[("B", *u, TILES[u][-1])])
                    last = o_last.get(o_before[u])
                    if last and last[0] == "y":
                        wait_tile(act, last)
                    elif last:
                        wait_read(act, last)
                    nc.scalar.activation(O[o_tile[u]][:, :], acc[:, :], ACT.Identity).then_inc(acc_out, 1)
                elif kind == "dsum":
                    wait_tile(act, s)
                    wait_sum_free(act, s)
                    nc.scalar.activation(DS[:, :], slot(s), ACT.Identity).then_inc(read_act, 1)
                elif kind == "y" and L == 0:
                    wait_tile(act, s)
                    if x_upd_before(s):
                        act.wait_ge(x_upd, x_upd_before(s))
                    nc.scalar.activation(T[:, :], slot(s), ACT.Identity).then_inc(read_act, 1)
                elif kind == "stats":
                    wait_x(act, L, b)
                    wait_norm_free(act, s)
                    if L == 2:
                        nc.scalar.activation(unused, X[b][:, :], ACT.Identity, scale=1.0 / N,
                                             accum_out=mv[:, 0, 0:1]).then_inc(act_chain, 1)
                        act.wait_ge(act_chain, b + 1)
                    nc.scalar.activation(unused, X[b][:, :], ACT.Square, scale=float(N) ** -0.5 if L == 2 else 1.0,
                                         accum_out=mv[:, 0, 1:2]).then_inc(squares_done, 1)
                elif kind == "norm":
                    act.wait_ge(coef_done, norm_no[s] + 1)
                    wait_norm_free(act, s)
                    for h in halves:
                        nc.scalar.activation(XN[:, h], X[b][:, h], ACT.Identity, scale=ab[:, 0, 0:1],
                                             bias=ab[:, 0, 1:2]).then_inc(xn_done if h.start else xn_half, 1)

        @block.vector
        def _(dve):
            links = [0]

            def link(ins):
                links[0] += 1
                ins.then_inc(dve_chain, 1)
                dve.wait_ge(dve_chain, links[0])

            nc.vector.memset(ST[0][:, 0:4, :].bitcast(F32), 0.0).then_inc(cleared_dve, 1)
            nc.vector.memset(eps[:, 0:1], EPS)
            link(nc.vector.memset(eps[:, 1:2], 16 * EPS))
            dve.wait_ge(w1_in, 16)
            nc.vector.tensor_tensor(lob[0][:, :], w("b0qk"), w("lo_sign"), ALU.mult).then_inc(signs_done, 1)
            for s in plan:
                kind, L, b = s[0], s[1], s[2] if len(s) > 2 else None
                if kind == "fold":
                    dve.wait_ge(w2_in, 16)
                    link(nc.vector.tensor_tensor(w("w0o").rearrange("p (h e) -> p h e", h=H0),
                                                 w("w0o").rearrange("p (h e) -> p h e", h=H0),
                                                 w("gam0").unsqueeze(2).broadcast_to([128, H0, 32]), ALU.mult))
                    nc.vector.tensor_tensor(gb0[:, :], w("gam0c"), w("b0o"), ALU.mult).then_inc(consts_ready, 1)
                    nc.vector.tensor_tensor(lob[1][:, :], w("b1qk"), w("lo_sign"), ALU.mult).then_inc(signs_done, 1)
                    nc.vector.tensor_tensor(gb1[:, :], w("gam1"), w("b1v"), ALU.mult).then_inc(consts_ready, 1)
                if kind in ("qk", "q", "k"):
                    if s not in half_no:
                        dve.wait_ge(hi_done, hi_no[s] + 1)
                        wait_tile(dve, s)
                        if b == 1:
                            dve.wait_ge(stacks_in[0], stacks_count(2, 0))
                        nc.vector.tensor_tensor(LK[:, :], slot(s)[:, 0:NKV], HK[:, :].bitcast(F32),
                                                ALU.subtract).then_inc(read_dve, 1)
                        continue
                    for h in halves:
                        if h.start == 0:
                            dve.wait_ge(half_full, half_no[s] + 1)
                            dve.wait_ge(hi_half, half_no[s] + 1)
                            if L == 3:
                                wait_ops_free(dve, L, b)
                            else:
                                wait_stage_free(dve, s)
                        else:
                            wait_tile(dve, s)
                            dve.wait_ge(hi_done, hi_no[s] + 1)
                        if kind == "qk":
                            lo = nc.vector.scalar_tensor_tensor(out=Ls[:, h], in0=slot(s)[:, h], scalar=w(f"b{L}qk"),
                                                                in1=Hs[:, h].bitcast(F32), op0=ALU.add, op1=ALU.add)
                        elif L == 2:
                            lo = nc.vector.tensor_tensor(Ls[:, h], slot(s)[:, h], Hs[:, h].bitcast(F32), ALU.subtract)
                        else:
                            k0 = 0 if kind == "q" else 8
                            lo = nc.vector.scalar_tensor_tensor(out=ST[b][:, k0 + 1, h], in0=slot(s)[:, h],
                                                                scalar=w("b3" + kind), in1=ST[b][:, k0, h].bitcast(F32),
                                                                op0=ALU.add, op1=ALU.subtract)
                    lo.then_inc(read_dve, 1)
                elif kind == "v" and L == 0:
                    wait_tile(dve, s)
                    dve.wait_ge(cleared_pool, 8)
                    nc.vector.tensor_tensor(
                        V0[b][:, :, :, 0:D0],
                        slot(s)[:, 0:NT * 16].rearrange("p (t h d) -> p h t d", t=NT, h=H0),
                        w("b0v").rearrange("p (h d) -> p h d", h=H0).unsqueeze(2).broadcast_to([128, H0, NT, D0]),
                        ALU.add).then_inc(read_dve, 1)
                elif kind == "A":
                    g, t = s[3], s[4]
                    u = split_no[("split", *s[1:4])]
                    wait_tile(dve, s)
                    if t == 0 and u >= 2:
                        dve.wait_ge(split_done, u - 1)
                    if L == 2:
                        nc.vector.tensor_reduce(out=NM[:, u % 2, 4 * t:4 * t + 4],
                                                in_=slot(s).rearrange("p (k r) -> p k r", k=4),
                                                op=ALU.max, axis=AX.X, negate=True).then_inc(read_dve, 1)
                    else:
                        nc.vector.tensor_reduce(out=NM[:, u % 2, t:t + 1], in_=slot(s), op=ALU.max, axis=AX.X,
                                                negate=True).then_inc(read_dve, 1)
                elif kind == "split":
                    u = split_no[s]
                    nk = 32 if L == 2 else 8
                    wait_read(dve, ("A", *s[1:4], 7))
                    if u >= 2:
                        wait_tile(dve, ("top", *list(split_no)[u - 2][1:]))
                    Z = ZT[:, u % 2, :, :].rearrange("p a k -> p (a k)")
                    link(nc.vector.tensor_copy(Z[:, 0:nk].bitcast(F32R), NM[:, u % 2, 0:nk]))
                    nc.vector.tensor_tensor(Z[:, nk:2 * nk], NM[:, u % 2, 0:nk], Z[:, 0:nk],
                                            ALU.subtract).then_inc(split_done, 1)
                elif kind == "den":
                    wait_tile(dve, s)
                    dve.wait_ge(cleared_pool, 14)
                    p = previous("bcast", s)
                    if p:
                        wait_tile(dve, p)
                    nc.vector.reciprocal(RR[:, :], slot(s)[0:64, 0:128]).then_inc(read_dve, 1)
                    wait_read(dve, s)
                    link(nc.vector.tensor_copy(RH[:, :], RR[:, :]))
                    nc.vector.scalar_tensor_tensor(out=RT[0:64, :], in0=RH[:, :].bitcast(F32), scalar=w("lo_rows")[0:64],
                                                   in1=RR[:, :], op0=ALU.mult, op1=ALU.add).then_inc(recip_done, 1)
                elif kind == "bcast":
                    g = s[3]
                    o = O[o_tile[(L, b, g)]]
                    wait_tile(dve, s)
                    if L == 0:
                        wait_read(dve, ("y", 0, b))
                        nc.vector.tensor_tensor(T[:, :], T[:, :], slot(s), ALU.mult).then_inc(read_dve, 1)
                        wait_read(dve, s)
                        dve.wait_ge(consts_ready, 1)
                        nc.vector.scalar_tensor_tensor(out=X[b][:, :], in0=T[:, :], scalar=gb0[:, 0:1], in1=X[b][:, :],
                                                       op0=ALU.add, op1=ALU.add).then_inc(x_upd, 1)
                    elif L == 2:
                        dve.wait_ge(acc_out, out_no[("out", L, b, g)] + 1)
                        nc.vector.tensor_tensor(o[:, :], o[:, :], slot(s), ALU.mult).then_inc(read_dve, 1)
                    else:
                        dve.wait_ge(acc_out, out_no[("out", L, b, g)] + 1)
                        if x_upd_before(s):
                            dve.wait_ge(x_upd, x_upd_before(s))
                        nc.vector.tensor_tensor(T[:, :], o[:, :], slot(s), ALU.mult).then_inc(read_dve, 1)
                        wait_read(dve, s)
                        if L == 1:
                            dve.wait_ge(consts_ready, 2)
                        else:
                            wait_read(dve, ("fold", 3))
                        nc.vector.scalar_tensor_tensor(out=X[b][:, :], in0=T[:, :],
                                                       scalar=gb1[:, 0:1] if L == 1 else b3eff[:, 0:1], in1=X[b][:, :],
                                                       op0=ALU.add, op1=ALU.add).then_inc(x_upd, 1)
                elif kind == "y" and L == 2:
                    wait_tile(dve, s)
                    nc.vector.tensor_tensor(X[b][:, :], slot(s), X[b][:, :], ALU.add).then_inc(read_dve, 1)
                elif kind == "out" and L in (1, 3) and s[3]:
                    u = s[1:]
                    dve.wait_ge(pv_done, pv_done_at[("B", *u, TILES[u][-1])])
                    o = O[o_tile[u]]
                    nc.vector.tensor_tensor(o[:, :], acc[:, :], o[:, :], ALU.add).then_inc(acc_out, 1)
                elif s in den_no and s[4] >= POOL_SUM:
                    sum_exps(nc.vector, dve, s)
                elif kind == "stats":
                    wait_x(dve, L, b)
                    wait_norm_free(dve, s)
                    if L == 3:
                        nc.vector.tensor_reduce(out=mv[:, 0, 0:1], in_=X[b][:, :], op=ALU.add,
                                                axis=AX.X).then_inc(stats_done, 1)
                        continue
                    xv = X[b][:, :].rearrange("c (m two) -> c m two", two=2)
                    link(nc.vector.tensor_tensor(KP, xv[:, :, 0], xv[:, :, 1], ALU.add))
                    kv2 = KP.rearrange("c (i two j) -> c i two j", two=2, j=16)
                    link(nc.vector.tensor_tensor(KV[:, :].rearrange("c (i j) -> c i j", j=16),
                                                 kv2[:, :, 0, :], kv2[:, :, 1, :], ALU.add))
                    link(nc.vector.bn_stats(bn[:, :], KV[:, :]))
                    link(nc.vector.bn_aggr(mv[:, 1, :], bn[:, :].unsqueeze(1)))
                    nc.vector.scalar_tensor_tensor(out=mv[:, 1, 1:2], in0=mv[:, 1, 0:1], scalar=mv[:, 1, 0:1],
                                                   in1=mv[:, 1, 1:2], op0=ALU.mult, op1=ALU.add).then_inc(stats_done, 1)
                elif kind == "norm":
                    ni = 2 if L == 2 else 1
                    wait_tile(dve, s)
                    nc.vector.tensor_scalar(gs[:, 0:ni, :], slot(s)[:, 0:2 * ni].rearrange("p (i k) -> p i k", k=2),
                                            -1.0, None, ALU.mult).then_inc(read_dve, 1)
                    wait_read(dve, s)
                    minus_v, y, a, h = (nt[:, i, 0:ni] for i in range(4))
                    gn = w(f"gn{L}").rearrange("p (i k) -> p i k", k=2)
                    cols = [slice(i, i + 1) for i in range(ni)]

                    def product(out, x, scalar, added, op=ALU.add):
                        for c in cols:
                            ins = nc.vector.scalar_tensor_tensor(out=out[:, c], in0=x[:, c], scalar=scalar[:, c],
                                                                 in1=added[:, c], op0=ALU.mult, op1=op)
                        return ins

                    link(product(minus_v, gs[:, :, 0], gs[:, :, 0], gs[:, :, 1]))
                    link(nc.vector.scalar_tensor_tensor(out=minus_v, in0=minus_v, scalar=0.0, in1=eps[:, 0:ni],
                                                        op0=ALU.min, op1=ALU.subtract))
                    nc.vector.tensor_scalar(h, minus_v, 0.5, None, ALU.mult)
                    link(nc.vector.tensor_scalar(y.bitcast(I32), minus_v.bitcast(I32), -0.5,
                                                 float(RSQRT_SEED - 2 ** 30), ALU.mult, ALU.add))
                    for _ in range(3):
                        link(product(a, y, h, y, ALU.mult))
                        link(nc.vector.scalar_tensor_tensor(out=y, in0=a, scalar=1.5, in1=y, op0=ALU.add, op1=ALU.mult))
                    if norm_no[s]:
                        dve.wait_ge(xn_done, norm_no[s])
                    link(nc.vector.tensor_tensor(ab[:, 0:ni, 0], y, gn[:, 0:ni, 0], ALU.mult))
                    product(ab[:, :, 1], gs[:, :, 0], ab[:, :, 0], gn[:, :, 1]).then_inc(coef_done, 1)
                    if L == 2:
                        dve.wait_ge(coef_done, norm_no[s] + 1)
                        if b == 1:
                            wait_tile(dve, ("v", 2, 0))
                        nc.vector.tensor_scalar(KVN[:, :], KV[:, :], ab[:, 1, 0:1], ab[:, 1, 1:2],
                                                ALU.mult, ALU.add).then_inc(kvn_done, 1)

        @block.tensor
        def _(pe):
            def full(s, mm):
                mm.then_inc(tile_full, 1)

            for s in plan:
                kind, L, b = s[0], s[1], s[2] if len(s) > 2 else None
                if kind == "ya":
                    s = ("y", L, b)
                if s in job and job[s] >= RING:
                    wait_read(pe, jobs[job[s] - RING])
                if kind == "fold":
                    pe.wait_ge(w2_in, 16)
                    nc.tensor.matmul(slot(s)[:, 0:C], w("w3v"), w("w3o"), start=True, stop=True)
                    full(s, nc.tensor.matmul(slot(s)[:, HALF:HALF + 1], w("w3o"), w("b3v"), start=True, stop=True))
                elif s[:2] == ("k", 2):
                    pe.wait_ge(kvn_done, b + 1)
                    full(s, nc.tensor.matmul(slot(s)[:, 0:NKV], w("w2k"), KVN[:, :], start=True, stop=True))
                elif kind in ("qk", "q", "k"):
                    src, wt = (X[b], w(f"w{L}qk")) if kind == "qk" else (XN, w(f"w{L}{kind}"))
                    if kind == "qk":
                        if L == 0:
                            pe.wait_ge(w1_in, 16)
                        wait_x(pe, L, b)
                    else:
                        pe.wait_ge(xn_half, norm_no[("norm", L, b)] + 1)
                    nc.tensor.matmul(slot(s)[:, halves[0]], wt, src[:, halves[0]], start=True,
                                     stop=True).then_inc(half_full, 1)
                    if kind != "qk":
                        pe.wait_ge(xn_done, norm_no[("norm", L, b)] + 1)
                    full(s, nc.tensor.matmul(slot(s)[:, halves[1]], wt, src[:, halves[1]], start=True, stop=True))
                elif kind == "v":
                    src, wv, width, tiles = {0: (X[b], w("w0v"), 16, NT), 1: (X[b], w("w1v"), C, NT),
                                             2: (KVN, w("w2v"), C, 2), 3: (XN, w3vo[:, :], C, NT)}[L]
                    if L == 3:
                        wait_read(pe, ("fold", 3))
                    for t in range(tiles):
                        mm = nc.tensor.matmul(slot(s)[:, width * t:width * (t + 1)], src[:, 128 * t:128 * (t + 1)], wv,
                                              start=True, stop=True)
                    full(s, mm)
                elif kind == "A":
                    g, t = s[3], s[4]
                    if t == 0:
                        pe.wait_ge(stacks_in[b], stacks_count(L, b))
                        if L == 2 and g == 1:
                            pe.wait_ge(stacks_late[b], 64)
                        if L == 2:
                            pe.wait_ge(cleared_pool, 19)
                    if L == 3:
                        wait_read(pe, ("q", 3, b))
                        wait_read(pe, ("k", 3, b))
                        for h in halves:
                            mm = nc.tensor.matmul(slot(s)[:, h], ST[b][:, 0, 128 * t:128 * (t + 1)], ST[b][:, 8, h],
                                                  start=True, stop=True)
                    elif L == 2:
                        head = HG * g + t // 2
                        k = ST[b][0:KROWS, 8:10, :].rearrange("p s n -> p (s n)")[:, NKV * head:NKV * (head + 1)]
                        for i in range(4):
                            kt = 4 * (t % 2) + i
                            mm = nc.tensor.matmul(slot(s)[:, NKV * i:NKV * (i + 1)],
                                                  ST[b][0:KROWS, head, 128 * kt:128 * (kt + 1)], k,
                                                  start=True, stop=True)
                    else:
                        ks, rs = (g, 4 + g) if L == 0 else (0, 4)
                        for h in halves:
                            mm = nc.tensor.matmul(slot(s)[:, h], ST[b][0:KROWS, ks, 128 * t:128 * (t + 1)],
                                                  ST[b][0:KROWS, rs, h], start=True, stop=True)
                    full(s, mm)
                elif kind == "top":
                    u = split_no[("split", *s[1:])]
                    nk = 32 if L == 2 else 8
                    pe.wait_ge(w2_in, 16)
                    pe.wait_ge(split_done, u + 1)
                    full(s, nc.tensor.transpose(slot(s)[0:2 * nk, 0:128],
                                                ZT[:, u % 2, :, :].rearrange("p a k -> p (a k)")[:, 0:2 * nk], w("ident")))
                elif kind == "B":
                    g, t = s[3], s[4]
                    if t == 0 and L != 3:
                        pe.wait_ge(maxrows_in[b], max_count(L, b, g))
                    if L == 3:
                        tile = slice(128 * t, 128 * (t + 1))
                        for i, (r, k) in enumerate(((8, 0), (8, 1), (9, 0), (9, 1))):
                            for h in halves:
                                nc.tensor.matmul(slot(s)[:, h], ST[b][:, r, tile], ST[b][:, k, h],
                                                 start=i == 0, stop=False)
                        if t == 0:
                            pe.wait_ge(cleared_pool, 19)
                            pe.wait_ge(maxrows_in[b], max_count(L, b, g))
                        for h in halves:
                            mm = nc.tensor.matmul(slot(s)[:, h], pick[:, :], ST[b][0:KROWS, 2, h],
                                                  start=False, stop=True)
                    else:
                        if L == 2:
                            head, rt = HG * g + t % 4, t // 4
                            ks = head
                            red = ST[b][0:KROWS, 8:10, :].rearrange("p s n -> p (s n)")[
                                :, NKV * head + 128 * rt:NKV * head + 128 * (rt + 1)]
                        else:
                            ks = g if L == 0 else 0
                            red = ST[b][0:KROWS, 4 + ks, 128 * t:128 * (t + 1)]
                        for h in halves:
                            mm = nc.tensor.matmul(slot(s)[:, h], red, ST[b][0:KROWS, ks, h], start=True, stop=True)
                    full(s, mm)
                elif kind in ("PV4", "PV1"):
                    g, t0, h = s[3], s[4], halves[s[5]]
                    first, last = TILES[s[1:4]][0], TILES[s[1:4]][-1]
                    if t0 == (0 if kind == "PV4" else first) and s[5] == 0:
                        if out_no[("out", L, b, g)]:
                            pe.wait_ge(acc_out, out_no[("out", L, b, g)])
                        wait_read(pe, ("v", L, b))
                    if kind == "PV4":
                        tiles = [("B", L, b, g, 4 * t0 + j) for j in range(4)]
                        wait_read(pe, tiles[3])
                        for j, q in enumerate(tiles):
                            lhs = V0[b][:, g, 4 * t0 + j, :] if L == 0 else V2[b][:, g, t0, j, :]
                            mm = nc.tensor.matmul(acc[32 * j:32 * j + 32, h], lhs, P[:, b_no[q] % NP, h],
                                                  start=t0 == 0, stop=t0 == 1)
                    else:
                        q = ("B", L, b, g, t0)
                        wait_read(pe, q)
                        mm = nc.tensor.matmul(acc[:, h], V13[b][:, t0, :], P[:, b_no[q] % NP, h],
                                              start=t0 == first, stop=t0 == last)
                    if s[5] == 1:
                        mm.then_inc(pv_done, 1)
                elif kind == "den":
                    g = s[3]
                    if L == 0:
                        wait_read(pe, ("dsum", 0, b))
                    elif L == 2:
                        pe.wait_ge(acc_out, out_no[("out", L, b, g)] + 1)
                    else:
                        pe.wait_ge(den_acc, den_no[("PV1", L, b, g, 7, 0)])
                    src, sel = {0: (DS, w("pick4")), 1: (DS, w("ones4")), 2: (O[o_tile[(L, b, g)]], w("sel2")),
                                3: (DS, w("ones4"))}[L]
                    for t in range(NT):
                        mm = nc.tensor.matmul(slot(s)[0:64, 0:128], sel[:, 28 - 4 * t:92 - 4 * t],
                                              src[:, 128 * t:128 * (t + 1)], start=t == 0, stop=t == NT - 1)
                    full(s, mm)
                elif kind == "bcast":
                    pe.wait_ge(recip_done, recip_no[("den", *s[1:])] + 1)
                    pe.wait_ge(consts_act, 1)
                    for t in range(NT):
                        mm = nc.tensor.matmul(slot(s)[:, 128 * t:128 * (t + 1)], selr[:, t, :], RT[:, :],
                                              start=True, stop=True)
                    full(s, mm)
                elif kind == "dsum":
                    pe.wait_ge(w2_in, 16)
                    pe.wait_ge(acc_out, out_no[("out", 0, b, 3)] + 1)
                    for h in halves:
                        for i in range(H0):
                            mm = nc.tensor.matmul(slot(s)[32 * i:32 * i + 32, h], w("den0"), O[o_tile[(0, b, i)]][:, h],
                                                  start=True, stop=True)
                    full(s, mm)
                elif kind == "y" and L == 0:
                    pe.wait_ge(consts_ready, 1)
                    pe.wait_ge(acc_out, out_no[("out", 0, b, 3)] + 1)
                    for h in halves:
                        for i in range(H0):
                            mm = nc.tensor.matmul(slot(s)[32 * i:32 * i + 32, h], w("w0o")[:, 32 * i:32 * i + 32],
                                                  O[o_tile[(0, b, i)]][:, h], start=True, stop=True)
                    full(s, mm)
                elif kind in ("ya", "y"):
                    g = 0 if kind == "ya" else 1
                    wait_read(pe, ("bcast", 2, b, g))
                    for h in halves:
                        mm = nc.tensor.matmul(slot(s)[:, h], w("w2p")[:, 128 * g:128 * (g + 1)],
                                              O[o_tile[(2, b, g)]][:, h], start=g == 0, stop=g == 1)
                    if g == 1:
                        full(s, mm)
                elif kind == "norm":
                    pe.wait_ge(stats_done, norm_no[s] + 1)
                    pe.wait_ge(squares_done, norm_no[s] + 1)
                    ni = 2 if L == 2 else 1
                    full(s, nc.tensor.matmul(slot(s)[:, 0:2 * ni], w("avg16" if L == 2 else "avg4"),
                                             mv[:, 0:ni, :].rearrange("p i k -> p (i k)"), start=True, stop=True))


def pack(layout, parts):
    import numpy as np

    at, n = columns(layout)
    out = np.zeros((128, n), np.float32)
    for name, a in parts.items():
        out[:a.shape[0], at[name][0]:at[name][0] + a.shape[1]] = a
    return out


def kernel(**inputs):
    import numpy as np
    import concourse.bacc as bacc
    from concourse.bass_utils import run_bass_kernel_spmd

    a = {k: np.asarray(v) for k, v in inputs.items()}

    def col(v):
        return v.reshape(-1, 1)

    def dh(wt, h, d):
        return wt.reshape(h, d, C).transpose(1, 0, 2).reshape(h * d, C)

    def dhb(bias, h, d):
        return bias.reshape(h, d).transpose(1, 0).reshape(-1)

    w0qk = np.concatenate([dh(a["L0_conv_Wk"], H0, D0)] * 4 + [dh(a["L0_conv_Wq"], H0, D0)] * 4).T
    b0qk = col(np.concatenate([dhb(a["L0_conv_bk"], H0, D0)] * 4 + [dhb(a["L0_conv_bq"], H0, D0)] * 4))
    lo_sign = np.zeros((2, 4, 16, 1), np.float32)
    lo_sign[0, 1] = lo_sign[0, 3] = lo_sign[1, 2] = lo_sign[1, 3] = -1
    w0o = np.zeros((4, 32, H0, 32), np.float32)
    for j in range(4):
        w0o[j, 0:D0] = a["L0_conv_Wo"].transpose(2, 0, 1)
    den0 = np.zeros((4, 32, 32), np.float32)
    den0[:, D0] = 1

    def window(m):
        z = np.zeros((128, 92), np.float32)
        z[:, 28:32] = z[:, 60:64] = m
        return z

    pick4 = np.zeros((4, 32, 4), np.float32)
    for h in range(4):
        pick4[h, 0, h] = 1
    gam0 = a["L0_conv_gamma"]
    first = pack(FIRST, {
        "w0qk": w0qk, "b0qk": b0qk,
        "w0v": a["L0_conv_Wv"].reshape(16, C).T,
        "b0v": np.broadcast_to(a["L0_conv_bv"].reshape(1, 16), (128, 16)),
        "lo_sign": lo_sign.reshape(128, 1)})
    sel = np.zeros((NT, 4, NT, 4, 32), np.float32)
    for t in range(NT):
        for h in range(4):
            sel[t, h, t, h] = 1
    selp = np.zeros((128, 1024), np.float32)
    selp[0:32] = selp[32:64] = sel.reshape(32, 1024)
    w2p = np.zeros((HG, 32, 2, C), np.float32)
    w2p[:, 0:D2] = a["L2_conv_wproj"].T.reshape(2, HG, D2, C).transpose(1, 2, 0, 3)
    sel2 = np.zeros((HG, 32, HG), np.float32)
    for h in range(HG):
        sel2[h, D2, h] = 1
    qkv, qkvb = a["L3_conv_qkv_w"], a["L3_conv_qkv_b"]

    def blocks(n):
        m = np.zeros((C // n, n, C // n, n), np.float32)
        for i in range(C // n):
            m[i, :, i, :] = 1.0 / n
        return m.reshape(C, C)

    rest = pack(REST, {
        "gam0": np.broadcast_to(gam0.reshape(1, 4), (128, 4)),
        "gam0c": col(np.repeat(gam0, 32)), "b0o": col(a["L0_conv_bo"]),
        "w0o": w0o.reshape(128, 128), "ident": np.eye(128, dtype=np.float32),
        "den0": den0.reshape(128, 32), "pick4": window(pick4.reshape(128, 4)),
        "w1qk": np.concatenate([a["L1_conv_wq"]] * 4 + [a["L1_conv_wk"]] * 4).T,
        "b1qk": col(np.concatenate([a["L1_conv_bq"]] * 4 + [a["L1_conv_bk"]] * 4)),
        "w1v": a["L1_conv_wv"].T, "b1v": col(a["L1_conv_bv"]),
        "gam1": np.broadcast_to(a["L1_conv_gamma"].reshape(1, 1), (128, 1)),
        "w2q": np.concatenate([dh(m, HG, D2) for m in np.split(a["L2_conv_wq"], 2)]).T,
        "w2k": dh(a["L2_conv_wk"], H2, D2).T, "w2v": a["L2_conv_wv"].T,
        "w2p": w2p.reshape(128, 256),
        "gn2": np.stack([a["L2_conv_gnq_w"], a["L2_conv_gnq_b"], a["L2_conv_gnk_w"], a["L2_conv_gnk_b"]], 1),
        "avg16": blocks(16), "sel2": window(sel2.reshape(128, 4)), "ones4": window(np.ones((128, 4), np.float32)),
        "lo_rows": col(np.repeat(np.float32([0, -1, 0, 0]), 32)),
        "w3q": qkv[0:C].T, "w3k": qkv[C:2 * C].T, "w3v": qkv[2 * C:], "w3o": a["L3_conv_out_w"].T,
        "b3q": col(qkvb[0:C]), "b3k": col(qkvb[C:2 * C]), "b3v": col(qkvb[2 * C:]), "b3o": col(a["L3_conv_out_b"]),
        "gn3": np.stack([a["L3_conv_gn_w"], a["L3_conv_gn_b"]], 1), "avg4": blocks(4) / np.float32(N)})
    x = np.ascontiguousarray(a["x"]).reshape(B, C, N)

    nc = bacc.Bacc("TRN2", target_bir_lowering=False, num_devices=1)
    arrays = {"x": x, "w_first": first, "w_rest": rest, "row_selector": selp}
    args = [nc.dram_tensor(n, v.shape, F32, kind="ExternalInput").ap() for n, v in arrays.items()]
    out = nc.dram_tensor("y", (B, C, N), F32, kind="ExternalOutput").ap()
    attention_layers(nc, *args, out)
    r = run_bass_kernel_spmd(nc, [arrays], core_ids=[0])
    return r.results[0]["y"].reshape(B, C, 32, 32)
```
